# Optimizing a Trainium2 kernel written in Bass

```python
import numpy as np
import jax
import jax.numpy as jnp

def _softmax(x, axis=-1):
    return jax.nn.softmax(x, axis=axis)

def _gelu(x):
    return jax.nn.gelu(x, approximate=True)

def _silu(x):
    return jax.nn.silu(x)

def _sigmoid(x):
    return jax.nn.sigmoid(x)

def _layernorm(x, axis=-1, eps=1e-05):
    m = jnp.mean(x, axis=axis, keepdims=True)
    v = jnp.var(x, axis=axis, keepdims=True)
    return (x - m) / jnp.sqrt(v + eps)

def _scatter_add(tgt, idx, src, axis=0):
    return tgt.at[idx].add(src)

def _segment_sum(src, seg, n):
    return jax.ops.segment_sum(src, seg, n)
kernel_name = 'mk_gnn_preln_d1_gnn_r8_4cb004'

def setup_inputs(seed: int=0):
    np.random.seed(seed)
    _w = jnp.asarray

    def _rec_inputs():
        import jax
        import jax.numpy as jnp
        _gk = jax.random.key(seed)
        x = -0.0001006 + 1 * jax.random.normal(jax.random.fold_in(_gk, 1), (6250, 96), jnp.float32)
        src = jax.random.randint(jax.random.fold_in(_gk, 2), (100000,), 0, 6250, jnp.int32)
        dst = jnp.minimum((6250 * jax.random.uniform(jax.random.fold_in(_gk, 3), (100000,)) ** 2.0).astype(jnp.int32), 49999)
        _o = jnp.argsort(dst, stable=True)
        src = src[_o]
        dst = dst[_o]
        edge_attr_4 = 0.000714719 + 1.00021 * jax.random.normal(jax.random.fold_in(_gk, 11), (100000, 4), jnp.float32)
        return (x, src, dst, edge_attr_4)
    x, src, dst, edge_attr_4 = _rec_inputs()

    def _L0_gnn_setup():
        import jax, jax.numpy as jnp
        import numpy as np
        EPS = 1e-05

        def _mlp(h, W, b, gamma, beta):
            h = jax.nn.relu(h @ W + b)
            mu = jnp.mean(h, axis=0)
            var = jnp.mean(jnp.square(h - mu), axis=0)
            return gamma * (h - mu) * jax.lax.rsqrt(var + EPS) + beta
        key = jax.random.key(seed)
        ks = jax.random.split(key, 10)
        N, E, C_in, C_out, E_dim = (6250, 100000, 96, 96, 4)
        x = jax.random.normal(ks[0], (N, C_in), dtype=jnp.float32)
        edge_index = jax.random.randint(ks[1], (2, E), 0, N, dtype=jnp.int64)
        edge_attr = jax.random.normal(ks[2], (E, E_dim), dtype=jnp.float32)
        s = lambda fan_in: 1.0 / np.sqrt(fan_in)
        W_node = jax.random.uniform(ks[3], (C_in, C_out), jnp.float32, -s(C_in), s(C_in))
        b_node = jnp.zeros((C_out,), jnp.float32)
        g_node = jnp.ones((C_out,), jnp.float32)
        beta_node = jnp.zeros((C_out,), jnp.float32)
        W_edge = jax.random.uniform(ks[4], (E_dim, C_out), jnp.float32, -s(E_dim), s(E_dim))
        b_edge = jnp.zeros((C_out,), jnp.float32)
        g_edge = jnp.ones((C_out,), jnp.float32)
        beta_edge = jnp.zeros((C_out,), jnp.float32)
        M_in = 2 * C_in + C_out
        W_msg = jax.random.uniform(ks[5], (M_in, C_out), jnp.float32, -s(M_in), s(M_in))
        b_msg = jnp.zeros((C_out,), jnp.float32)
        g_msg = jnp.ones((C_out,), jnp.float32)
        beta_msg = jnp.zeros((C_out,), jnp.float32)
        return dict(x=x, edge_index=edge_index, edge_attr=edge_attr, W_node=W_node, b_node=b_node, g_node=g_node, beta_node=beta_node, W_edge=W_edge, b_edge=b_edge, g_edge=g_edge, beta_edge=beta_edge, W_msg=W_msg, b_msg=b_msg, g_msg=g_msg, beta_msg=beta_msg)
    _L0_gnn_all = _L0_gnn_setup()
    _L0_gnn_in = {k: v for k, v in _L0_gnn_all.items() if k in ('W_node', 'b_node', 'g_node', 'beta_node', 'W_edge', 'b_edge', 'g_edge', 'beta_edge', 'W_msg', 'b_msg', 'g_msg', 'beta_msg')}
    del _L0_gnn_all
    return {'x': x, 'src': src, 'dst': dst, 'edge_attr_4': edge_attr_4, 'L0_gnn_W_node': _L0_gnn_in['W_node'], 'L0_gnn_b_node': _L0_gnn_in['b_node'], 'L0_gnn_g_node': _L0_gnn_in['g_node'], 'L0_gnn_beta_node': _L0_gnn_in['beta_node'], 'L0_gnn_W_edge': _L0_gnn_in['W_edge'], 'L0_gnn_b_edge': _L0_gnn_in['b_edge'], 'L0_gnn_g_edge': _L0_gnn_in['g_edge'], 'L0_gnn_beta_edge': _L0_gnn_in['beta_edge'], 'L0_gnn_W_msg': _L0_gnn_in['W_msg'], 'L0_gnn_b_msg': _L0_gnn_in['b_msg'], 'L0_gnn_g_msg': _L0_gnn_in['g_msg'], 'L0_gnn_beta_msg': _L0_gnn_in['beta_msg']}

def reference(x, src, dst, edge_attr_4, L0_gnn_W_node, L0_gnn_b_node, L0_gnn_g_node, L0_gnn_beta_node, L0_gnn_W_edge, L0_gnn_b_edge, L0_gnn_g_edge, L0_gnn_beta_edge, L0_gnn_W_msg, L0_gnn_b_msg, L0_gnn_g_msg, L0_gnn_beta_msg):
    import jax
    import jax.numpy as jnp

    def _L0_gnn_ref(x, edge_index, edge_attr, W_node, b_node, g_node, beta_node, W_edge, b_edge, g_edge, beta_edge, W_msg, b_msg, g_msg, beta_msg):
        import jax, jax.numpy as jnp
        import numpy as np
        EPS = 1e-05

        def _mlp(h, W, b, gamma, beta):
            h = jax.nn.relu(h @ W + b)
            mu = jnp.mean(h, axis=0)
            var = jnp.mean(jnp.square(h - mu), axis=0)
            return gamma * (h - mu) * jax.lax.rsqrt(var + EPS) + beta
        node_feat = _mlp(x, W_node, b_node, g_node, beta_node)
        edge_feat = _mlp(edge_attr, W_edge, b_edge, g_edge, beta_edge)
        row, col = (edge_index[0], edge_index[1])
        message = jnp.concatenate([x[row], x[col], edge_feat], axis=1)
        message = _mlp(message, W_msg, b_msg, g_msg, beta_msg)
        agg = jax.ops.segment_sum(message, col, num_segments=node_feat.shape[0])
        return agg + node_feat
    edge_index = jnp.stack([src, dst])
    h = jnp.maximum(_layernorm(x, axis=-1), 0.0)
    x = x + _L0_gnn_ref(h, edge_index, edge_attr_4, L0_gnn_W_node, L0_gnn_b_node, L0_gnn_g_node, L0_gnn_beta_node, L0_gnn_W_edge, L0_gnn_b_edge, L0_gnn_g_edge, L0_gnn_beta_edge, L0_gnn_W_msg, L0_gnn_b_msg, L0_gnn_g_msg, L0_gnn_beta_msg)
    return x

_drawn_inputs = setup_inputs


def setup_inputs(seed=0):
    import zlib

    import numpy as np

    out = dict(_drawn_inputs(seed))
    spreads = {'L0_gnn_b_node': (0.0, 0.576),
     'L0_gnn_g_node': (1.0, 0.6),
     'L0_gnn_beta_node': (0.0, 0.8),
     'L0_gnn_b_edge': (0.0, 0.1),
     'L0_gnn_g_edge': (1.0, 0.2),
     'L0_gnn_beta_edge': (0.0, 0.286),
     'L0_gnn_b_msg': (0.0, 0.1),
     'L0_gnn_g_msg': (1.0, 0.2),
     'L0_gnn_beta_msg': (0.0, 0.1)}
    factors = {}
    for name, (base, spread) in spreads.items():
        noise = np.random.default_rng([zlib.crc32(name.encode()), seed]).standard_normal(out[name].shape)
        drawn = base * np.exp(spread * noise) if base else spread * noise
        out[name] = jnp.asarray(drawn.astype(out[name].dtype))
    for name, factor in factors.items():
        out[name] = (out[name] * factor).astype(out[name].dtype)
    return out
```

```python
import concourse.bass as bass
from concourse import mybir
from contextlib import ExitStack

N, E, C, EF = 6250, 100000, 96, 4
P = 128
TILE = P
TPG = 4
GROUP = TPG * TILE
NG = -(-E // GROUP)
NTILES = NG * TPG
LAST_EDGES = E - (NG - 1) * GROUP
LAST_TILES = -(-LAST_EDGES // TILE)
LAST_ROWS = LAST_EDGES - (LAST_TILES - 1) * TILE
EP = NG * GROUP
WIN = 96
NB = -(-(N + WIN) // P)
NP = NB * P
NQ = -(-NB // 4)
EPS = 1e-5
STACK = (("hi", "hi"), ("hi", "mid"), ("hi", "lo"), ("mid", "hi"), ("mid", "mid"), ("lo", "hi"))
EROWS = EF + 1
KROWS = len(STACK) * EROWS
SPLIT_F = EROWS * EP // P
BODY = 4
LOOPS = NG // BODY
RING = 48
ROUNDS = (NG - BODY) // RING
AHEAD = 3
HALF = RING // 2 * TPG
IDX_W = (ROUNDS * RING + AHEAD) * TPG + HALF
LN_CHUNK = 10
GEN_WINS = -(-N // WIN)
M1 = C + 1
MW = C + 1 + C


def graph_layer(nc, x_nodes, x_t, src_cols, dst_cols, group_base, edge_rows, w_node, b_node, g_node, beta_node,
                w_edge, b_edge, g_edge, beta_edge, w_msg, b_msg, g_msg, beta_msg, ident_in, ramp_in, out_t):
    fp32, bf16, i32 = mybir.dt.float32, mybir.dt.bfloat16, mybir.dt.int32
    ALU, ACT, AX = mybir.AluOpType, mybir.ActivationFunctionType, mybir.AxisListType.X

    p_table = nc.dram_tensor("p_table", (NP, C), fp32, kind="Internal").ap()
    q_table = nc.dram_tensor("q_table", (NP, C), fp32, kind="Internal").ap()
    x_stack = nc.dram_tensor("x_stack", (KROWS, EP), bf16, kind="Internal").ap()

    with ExitStack() as ctx:
        def sb(name, shape, dt=fp32):
            return ctx.enter_context(nc.sbuf_tensor(name, shape, dt))

        def sem(name):
            return ctx.enter_context(nc.semaphore(name))

        ring = sb("ring", [P, RING * TPG * C])
        node_slot = RING - -(-NB // TPG)
        node_at = RING * TPG * C - NB * C
        zn = ring[:, node_at:].rearrange("p (b c) -> p b c", c=C)
        big_a = sb("big_a", [P, NP])
        h_t, agg = big_a[0:C, :], big_a[0:M1, :]
        big_b = sb("big_b", [P, N])
        node_t, edge_f = big_b[0:C, :], big_b[:, 0:SPLIT_F]
        big_c = sb("big_c", [P, N])
        splits = big_c[:, 0:3 * SPLIT_F // 2].bitcast(bf16).rearrange("p (s f) -> p s f", s=3)
        res_t = big_c[0:C, :]
        xs = sb("xs", [KROWS, 4, 2 * GROUP], bf16)
        src_i = sb("src_i", [P, IDX_W], i32)
        idx_buf = sb("idx_buf", [P, 2, HALF], i32)
        dst_rel = sb("dst_rel", [P, NG, TPG])
        base_b = sb("base_b", [P, NG], i32)
        hot = sb("hot", [P, 4, TPG, WIN])
        dst_i = hot[:, :, :, :].bitcast(i32).rearrange("p a t w -> p (a t w)")
        dst_i2 = hot[:, 2:4, :, :].bitcast(i32).rearrange("p a t w -> p (a t w)")
        r_sb = sb("r_sb", [M1, 2, GROUP])
        hot_n = sb("hot_n", [WIN, 2, GROUP])
        msg = sb("msg", [P, 2, TPG, MW])
        acc = sb("acc", [P, TPG, MW])
        edge_st = sb("edge_st", [C, NG, 6])
        node_st = sb("node_st", [C, NQ, 6])
        ln_st = sb("ln_st", [P, NB, 6])
        ln_w = sb("ln_w", [P, 5, NB])
        q_win = sb("q_win", [WIN, 4, C])
        ident = sb("ident", [P, P])
        ramp = sb("ramp", [P, WIN])
        ones = sb("ones", [P, 1])
        wn = sb("wn", [C, C])
        w1 = sb("w1", [C, C])
        w2 = sb("w2", [C, C])
        w3 = sb("w3", [C, C])
        w3c = sb("w3c", [M1, C])
        bm_row = sb("bm_row", [M1, C])
        we5 = sb("we5", [EROWS, M1])
        we_split = sb("we_split", [EROWS, 3, M1], bf16)
        we_stack = sb("we_stack", [KROWS, M1], bf16)
        vec = sb("vec", [C, 8])
        sc = sb("sc", [C, 16])
        t_col = sb("t_col", [C, M1])
        fold = sb("fold", [C, M1])
        s_diag = sb("s_diag", [M1, C])
        bad = sb("bad", [P, 4])
        flag = sb("flag", [1, 1], i32)
        ln_rstd, ln_mean = ln_w[:, 3, :], ln_w[:, 4, :]

        pa = ctx.enter_context(nc.psum_tensor("pa", [P, 2, 512], fp32))
        pb = ctx.enter_context(nc.psum_tensor("pb", [P, 2, 512], fp32))
        pc = ctx.enter_context(nc.psum_tensor("pc", [P, 2, 512], fp32))
        pd = ctx.enter_context(nc.psum_tensor("pd", [P, 2, 512], fp32))

        B_NODE, G_NODE, BT_NODE, G_EDGE, BT_EDGE, G_MSG, BT_MSG = range(7)

        x_in = [sem(f"x_in{c}") for c in range(NB // LN_CHUNK)]
        edge_in = sem("edge_in")
        consts_in = sem("consts_in")
        dst_in = sem("dst_in")
        src_in = sem("src_in")
        zeroed = sem("zeroed")
        dve_step = sem("dve_step")
        ln_var = sem("ln_var")
        ln_sqrt = sem("ln_sqrt")
        z_ready = sem("z_ready")
        z_turned = sem("z_turned")
        h_kept = sem("h_kept")
        p_made = sem("p_made")
        p_kept = sem("p_kept")
        p_stored = sem("p_stored")
        q_made = sem("q_made")
        q_kept = sem("q_kept")
        q_stored = sem("q_stored")
        node_made = sem("node_made")
        node_relu = sem("node_relu")
        split_step = sem("split_step")
        stack_stored = sem("stack_stored")
        we_ready = sem("we_ready")
        we_placed = sem("we_placed")
        bad_ready = sem("bad_ready")
        bad_counted = sem("bad_counted")
        flag_ready = sem("flag_ready")
        res_in = sem("res_in")
        sqrt_asked = sem("sqrt_asked")
        sqrt_done = sem("sqrt_done")
        shift_ready = sem("shift_ready")
        shift_made = sem("shift_made")
        p1_x = [sem(f"p1_x{k}") for k in range(4)]
        p1_lin = sem("p1_lin")
        p1_relu = sem("p1_relu")
        p1_stat = sem("p1_stat")
        main_ready = sem("main_ready")
        idx_ready = sem("idx_ready")
        gather_done = [sem(f"gather_done{k}") for k in range(4)]
        gathered = sem("gathered")
        x_main = [sem(f"x_main{k}") for k in range(2)]
        q_in = [sem(f"q_in{k}") for k in range(4)]
        edge_lin = sem("edge_lin")
        edge_relu = sem("edge_relu")
        hot_built = sem("hot_built")
        hot_turned = sem("hot_turned")
        hot_kept = sem("hot_kept")
        pre_summed = sem("pre_summed")
        pre_added = sem("pre_added")
        msg_relu = sem("msg_relu")
        msg_square = sem("msg_square")
        win_summed = sem("win_summed")
        win_added = sem("win_added")
        acc_added = sem("acc_added")
        gen_turn = sem("gen_turn")
        gen_x = sem("gen_x")
        gen_idx = sem("gen_idx")
        gen_rows = sem("gen_rows")
        gen_claimed = sem("gen_claimed")
        gen_lin = sem("gen_lin")
        gen_relu = sem("gen_relu")
        gen_sum = sem("gen_sum")
        gen_dst = sem("gen_dst")
        gen_pre = sem("gen_pre")
        gen_msg = sem("gen_msg")
        gen_square = sem("gen_square")
        gen_hot = sem("gen_hot")
        gen_win = sem("gen_win")
        gen_step = sem("gen_step")
        messages_done = sem("messages_done")
        sums_made = sem("sums_made")
        fold_ready = sem("fold_ready")
        fold_turned = sem("fold_turned")
        diag_kept = sem("diag_kept")
        out_made = sem("out_made")
        out_ready = sem("out_ready")
        out_stored = sem("out_stored")

        def at(i, j):
            return i + j // BODY, j % BODY

        def num(i, j):
            return i * BODY + j

        def exists(i, j):
            return not isinstance(i, int) or 0 <= num(i, j) < NG

        def wait(eng, s, value):
            if not isinstance(value, int) or value > 0:
                eng.wait_ge(s, value)

        def tiles(i, j):
            return LAST_TILES if isinstance(i, int) and num(i, j) == NG - 1 else TPG

        def passes(eng, body):
            body(0)
            with eng.Fori(1, LOOPS - 1) as i:
                body(i)
            body(LOOPS - 1)

        def quad(q):
            return min(4, NB - 4 * q)

        def nodes(q):
            return min(512, N - 512 * q)

        consts = [(ident[:, :], ident_in), (ramp[:, :], ramp_in), (wn[:, :], w_node), (w1[:, :], w_msg[0:C, :]),
                  (w2[:, :], w_msg[C:2 * C, :]), (w3[:, :], w_msg[2 * C:3 * C, :]), (bm_row[C:M1, :], b_msg),
                  (vec[:, B_NODE:B_NODE + 1], b_node), (vec[:, G_NODE:G_NODE + 1], g_node),
                  (vec[:, BT_NODE:BT_NODE + 1], beta_node), (vec[:, G_EDGE:G_EDGE + 1], g_edge),
                  (vec[:, BT_EDGE:BT_EDGE + 1], beta_edge), (vec[:, G_MSG:G_MSG + 1], g_msg),
                  (vec[:, BT_MSG:BT_MSG + 1], beta_msg)]
        N_CONSTS = 16 * (len(consts) + 2)

        block = ctx.enter_context(nc.Block())

        @block.sync
        def _(sp):
            def stack_rows(k):
                rows = x_stack[k * EROWS:(k + 1) * EROWS, :].rearrange("r e -> (r e)")
                return rows.rearrange("(p f) -> p f", p=P)

            for c in range(NB // LN_CHUNK):
                b0 = c * LN_CHUNK
                sp.dma_start(zn[:, b0:b0 + LN_CHUNK, :], x_nodes[:, b0:b0 + LN_CHUNK, :]).then_inc(x_in[c], 16)
                if c == 0:
                    sp.dma_start(edge_f, edge_rows).then_inc(edge_in, 16)
            for s, name in ((0, "hi"), (1, "mid")):
                sp.wait_ge(split_step, (1, 3)[s])
                for k, (part, _) in enumerate(STACK):
                    if part == name:
                        sp.dma_start(stack_rows(k), splits[:, s, :]).then_inc(stack_stored, 16)
            for q in range(NQ):
                sp.wait_ge(p_kept, q + 1)
                sp.dma_start(p_table[512 * q:512 * q + 128 * quad(q), :].rearrange("(b p) c -> p b c", p=P),
                             zn[:, 4 * q:4 * q + quad(q), :]).then_inc(p_stored, 16)
            sp.wait_ge(split_step, 5)
            k = len(STACK) - 1
            sp.dma_start(stack_rows(k), splits[:, 2, :]).then_inc(stack_stored, 16)
            for q in range(NQ):
                sp.wait_ge(q_kept, q + 1)
                sp.dma_start(q_table[512 * q:512 * q + 128 * quad(q), :].rearrange("(b p) c -> p b c", p=P),
                             zn[:, 4 * q:4 * q + quad(q), :]).then_inc(q_stored, 16)
            sp.wait_ge(stack_stored, 16 * len(STACK))

            def load_p1(i, units):
                for k in range(units):
                    u = i * 4 + k
                    wait(sp, p1_lin, u * 2 - 6)
                    sp.dma_start(xs[:, k, :], x_stack[:, bass.ts(u, 2 * GROUP)]).then_inc(p1_x[k], 16)

            load_p1(0, 4)
            with sp.Fori(1, NG // 8) as i:
                load_p1(i, 4)
            load_p1(NG // 8, (NG % 8) // 2)
            sp.dma_start(res_t, x_t).then_inc(res_in, 16)

            sp.wait_ge(p1_lin, NG)
            sp.wait_ge(q_stored, 16 * NQ)
            sp.wait_ge(flag_ready, 1)
            outside = sp.value_load(flag[0:1, 0:1], min_val=0, max_val=2 * P)
            with sp.If(outside < 1):
                def fast(i):
                    for j in range(BODY):
                        g = num(i, j)
                        if j % 2 == 0:
                            wait(sp, edge_lin, g - 2)
                            sp.dma_start(xs[:, j // 2, :], x_stack[:, bass.ds(g * GROUP, 2 * GROUP)]).then_inc(
                                x_main[j // 2], 16)
                        wait(sp, pre_summed, g - 3)
                        base = sp.value_load(base_b[0:1, bass.ds(g, 1)], min_val=0, max_val=N - 1)
                        sp.dma_start(q_win[:, j, :], q_table[bass.ds(base, WIN), :]).then_inc(q_in[j], 16)
                passes(sp, fast)
            with sp.Else():
                with sp.Fori(0, NG) as g:
                    sp.wait_ge(gen_turn, g + 1)
                    sp.dma_start(xs[:, 0, 0:GROUP], x_stack[:, bass.ds(g * GROUP, GROUP)]).then_inc(gen_x, 16)
                    sp.dma_start(dst_i2[:, 0:TPG], dst_cols[:, bass.ds(g * TPG, TPG)]).then_inc(gen_dst, 16)

            for q in range(NQ):
                sp.wait_ge(out_ready, q + 1)
                sp.dma_start(out_t[:, 512 * q:512 * q + nodes(q)], node_t[:, 512 * q:512 * q + nodes(q)]).then_inc(
                    out_stored, 16)
            sp.wait_ge(out_stored, 16 * NQ)

        @block.gpsimd
        def _(pool):
            pool.wait_ge(edge_in, 16)
            nc.gpsimd.tensor_copy(splits[:, 0, :], edge_f).then_inc(split_step, 1)
            pool.wait_ge(split_step, 1)
            nc.gpsimd.tensor_tensor(edge_f, edge_f, splits[:, 0, :], ALU.subtract).then_inc(split_step, 1)
            pool.wait_ge(split_step, 2)
            nc.gpsimd.tensor_copy(splits[:, 1, :], edge_f).then_inc(split_step, 1)
            pool.wait_ge(split_step, 3)
            nc.gpsimd.tensor_tensor(edge_f, edge_f, splits[:, 1, :], ALU.subtract).then_inc(split_step, 1)
            pool.wait_ge(split_step, 4)
            nc.gpsimd.tensor_copy(splits[:, 2, :], edge_f).then_inc(split_step, 1)

            def row_gather(slot, tile, table, idx, done):
                lo = (slot * TPG + tile) * C
                nc.gpsimd.indirect_dma_start(
                    out=ring[:, lo:lo + C], out_offset=None, in_=table,
                    in_offset=bass.IndirectOffsetOnAxis(ap=idx, axis=0)).then_inc(done, 16)

            pool.wait_ge(src_in, 16)
            nc.gpsimd.tensor_copy(idx_buf[:, 0, :], src_i[:, AHEAD * TPG:AHEAD * TPG + HALF]).then_inc(idx_ready, 1)
            pool.wait_ge(p_stored, 16 * NQ)
            pool.wait_ge(flag_ready, 1)
            outside = pool.value_load(flag[0:1, 0:1], min_val=0, max_val=2 * P)
            with pool.If(outside < 1):
                for g in range(AHEAD):
                    for t in range(TPG):
                        row_gather(g, t, p_table, src_i[:, g * TPG + t:g * TPG + t + 1], gather_done[g % 4])
                pool.wait_ge(idx_ready, 1)
                with pool.Fori(0, ROUNDS) as r:
                    for k in range(RING):
                        half, col = k // (RING // 2), k % (RING // 2) * TPG
                        slot = (k + AHEAD) % RING
                        if slot == node_slot:
                            pool.wait_ge(q_stored, 16 * NQ)
                        for t in range(TPG):
                            row_gather(slot, t, p_table, idx_buf[:, half, col + t:col + t + 1],
                                       gather_done[(k + AHEAD) % 4])
                        pool.wait_ge(gather_done[k % 4], r * (64 * RING // 4) + 64 * (k // 4 + 1))
                        if (k + 1) % (RING // 2) == 0:
                            pool.wait_ge(idx_ready, r * 2 + half + 2)
                        pool.wait_ge(pre_added, r * RING + (k + AHEAD + 2))
                        pool.sem_inc(gathered, 1)
                        if k % (RING // 2) == AHEAD:
                            start = (r * RING + (half + 1) * (RING // 2) + AHEAD) * TPG
                            nc.gpsimd.tensor_copy(idx_buf[:, 1 - half, :],
                                                  src_i[:, bass.ds(start, HALF)]).then_inc(idx_ready, 1)
                for g in range(ROUNDS * RING, NG):
                    if g + AHEAD < NG:
                        pool.wait_ge(pre_added, g + AHEAD + 1)
                        for t in range(tiles(0, g + AHEAD)):
                            col = (g + AHEAD) * TPG + t
                            row_gather((g + AHEAD) % RING, t, p_table, src_i[:, col:col + 1],
                                       gather_done[(g + AHEAD) % 4])
                    pool.wait_ge(gather_done[g % 4], 64 * (g // 4) + 16 * tiles(0, g))
                    pool.sem_inc(gathered, 1)
            with pool.Else():
                pool.wait_ge(q_stored, 16 * NQ)
                with pool.Fori(0, NG) as g:
                    pool.wait_ge(gen_turn, g + 1)
                    nc.gpsimd.tensor_copy(idx_buf[:, 0, 0:TPG], src_i[:, bass.ds(g * TPG, TPG)]).then_inc(gen_idx, 1)
                    pool.wait_ge(gen_dst, g * 16 + 16)
                    pool.wait_ge(gen_idx, g + 1)
                    pool.sem_inc(gen_claimed, 1)
                    for t in range(TPG):
                        row_gather(0, t, p_table, idx_buf[:, 0, t:t + 1], gen_rows)
                        row_gather(1, t, q_table, dst_i2[:, t:t + 1], gen_rows)

        @block.scalar
        def _(act):
            act.dma_start(dst_i[:, 0:NTILES], dst_cols).then_inc(dst_in, 16)
            act.dma_start(base_b[:, :], group_base.partition_broadcast(P)).then_inc(dst_in, 16)
            act.wait_ge(zeroed, 1)
            act.dma_start(we5[1:EROWS, 0:C], w_edge).then_inc(consts_in, 16)
            act.dma_start(we5[0:1, 0:C], b_edge).then_inc(consts_in, 16)
            for to, of in consts:
                act.dma_start(to, of).then_inc(consts_in, 16)
            act.dma_start(src_i[:, :], src_cols).then_inc(src_in, 16)
            for c in range(NB // LN_CHUNK):
                b = slice(c * LN_CHUNK, (c + 1) * LN_CHUNK)
                act.wait_ge(ln_var, c + 1)
                nc.scalar.sqrt(ln_w[:, 3, b], ln_w[:, 2, b]).then_inc(ln_sqrt, 1)
            act.wait_ge(we_ready, 1)
            for k, (_, part) in enumerate(STACK):
                act.dma_start(we_stack[k * EROWS:(k + 1) * EROWS, :],
                              we_split[:, ("hi", "mid", "lo").index(part), :]).then_inc(we_placed, 16)
            for q in range(NQ):
                act.wait_ge(z_turned, q + 1)
                nc.scalar.activation(h_t[:, 512 * q:512 * q + 128 * quad(q)], pb[0:C, q % 2, 0:128 * quad(q)],
                                     ACT.Relu).then_inc(h_kept, 1)
            for q in range(NQ):
                act.wait_ge(q_made, q + 1)
                if q == 0:
                    act.wait_ge(p_stored, 16 * NQ)
                nc.scalar.copy(zn[:, 4 * q:4 * q + quad(q), :].rearrange("p b c -> p (b c)"),
                               pc[:, q % 2, 0:C * quad(q)]).then_inc(q_kept, 1)
                act.wait_ge(node_made, q + 1)
                if q == 0:
                    act.wait_ge(split_step, 5)
                nc.scalar.activation(node_t[:, 512 * q:512 * q + nodes(q)], pb[0:C, q % 2, 0:nodes(q)], ACT.Relu,
                                     bias=vec[:, B_NODE:B_NODE + 1]).then_inc(node_relu, 1)

            def p1_group(g, k):
                act.wait_ge(p1_lin, g + 1)
                wait(act, p1_stat, g - 1)
                nc.scalar.activation(r_sb[0:C, k % 2, :], pa[0:C, k % 2, :], ACT.Relu).then_inc(p1_relu, 1)

            for k in range(8):
                p1_group(k, k)
            with act.Fori(1, NG // 8) as i:
                for k in range(8):
                    p1_group(i * 8 + k, k)
            for k in range(NG % 8):
                p1_group(NG // 8 * 8 + k, k)
            act.wait_ge(sqrt_asked, 1)
            nc.scalar.sqrt(sc[:, 4:6], sc[:, 2:4]).then_inc(sqrt_done, 1)

            act.wait_ge(flag_ready, 1)
            outside = act.value_load(flag[0:1, 0:1], min_val=0, max_val=2 * P)
            act.wait_ge(main_ready, 1)
            with act.If(outside < 1):
                def keep_edges(i, j):
                    i, j = at(i, j)
                    if not exists(i, j):
                        return
                    g, n = num(i, j), tiles(i, j) * TILE
                    act.wait_ge(edge_lin, g + 1)
                    wait(act, pre_summed, g - 1)
                    nc.scalar.activation(r_sb[:, j % 2, 0:n], pa[0:M1, j % 2, 0:n], ACT.Relu).then_inc(edge_relu, 1)
                    act.wait_ge(hot_turned, g + 1)
                    nc.scalar.copy(hot_n[:, j % 2, 0:n], pb[0:WIN, j % 2, 0:n]).then_inc(hot_kept, 1)

                def keep_messages(i, j):
                    i, j = at(i, j)
                    if not exists(i, j):
                        return
                    g, n = num(i, j), tiles(i, j)
                    wait(act, win_summed, g - 1)
                    wait(act, acc_added, g - 1)
                    act.wait_ge(pre_added, g + RING + 1)
                    nc.scalar.activation(msg[:, j % 2, 0:n, 0:C],
                                         pc[:, j % 2, 0:n * C].rearrange("p (t c) -> p t c", c=C),
                                         ACT.Relu).then_inc(msg_relu, 1)
                    act.wait_ge(msg_relu, g + 1)
                    nc.scalar.square(msg[:, j % 2, 0:n, M1:MW], msg[:, j % 2, 0:n, 0:C]).then_inc(msg_square, 1)

                keep_edges(0, 0)
                keep_edges(0, 1)
                keep_messages(0, 0)

                def fast(i):
                    for j in range(BODY):
                        keep_edges(i, j + 2)
                        keep_messages(i, j + 1)
                passes(act, fast)
            with act.Else():
                with act.Fori(0, NG) as g:
                    act.wait_ge(gen_lin, g + 1)
                    nc.scalar.activation(r_sb[:, 0, :], pa[0:M1, 0, :], ACT.Relu).then_inc(gen_relu, 1)
                    act.wait_ge(gen_pre, g + 1)
                    nc.scalar.activation(msg[:, 0, :, 0:C], pc[:, 0, 0:TPG * C].rearrange("p (t c) -> p t c", c=C),
                                         ACT.Relu).then_inc(gen_msg, 1)
                    act.wait_ge(gen_msg, g + 1)
                    nc.scalar.square(msg[:, 0, :, M1:MW], msg[:, 0, :, 0:C]).then_inc(gen_square, 1)

            act.wait_ge(sqrt_asked, 2)
            nc.scalar.sqrt(sc[:, 12:13], sc[:, 11:12]).then_inc(sqrt_done, 1)

        @block.tensor
        def _(pe):
            pe.wait_ge(consts_in, N_CONSTS)

            def turn(q):
                pe.wait_ge(z_ready, (4 * q + quad(q) - 1) // LN_CHUNK + 1)
                if q >= 2:
                    pe.wait_ge(h_kept, q - 1)
                for b in range(quad(q)):
                    last = nc.tensor.transpose(pb[0:C, q % 2, 128 * b:128 * b + 128], zn[:, 4 * q + b, :], ident[:, :])
                last.then_inc(z_turned, 1)

            def table(q, w, made, kept, before):
                pe.wait_ge(h_kept, q + 1)
                wait(pe, kept, q - 1)
                if before and q < 2:
                    pe.wait_ge(*before)
                for b in range(quad(q)):
                    n0 = 512 * q + 128 * b
                    last = nc.tensor.matmul(pc[:, q % 2, C * b:C * b + C], h_t[:, n0:n0 + 128], w[:, :],
                                            start=True, stop=True)
                last.then_inc(made, 1)

            turn(0)
            for q in range(NQ):
                if q + 1 < NQ:
                    turn(q + 1)
                table(q, w1, p_made, p_kept, None)
            pe.wait_ge(bad_ready, 1)
            nc.tensor.matmul(pd[0:1, 0, 0:2], ones[:, :], bad[:, 2:4], start=True, stop=True).then_inc(bad_counted, 1)
            for q in range(NQ):
                table(q, w2, q_made, q_kept, (p_kept, NQ))
                wait(pe, node_relu, q - 1)
                nc.tensor.matmul(pb[0:C, q % 2, 0:nodes(q)], wn[:, :], h_t[:, 512 * q:512 * q + nodes(q)],
                                 start=True, stop=True).then_inc(node_made, 1)

            pe.wait_ge(we_placed, 16 * len(STACK))

            def p1_group(g, k, i):
                if k % 2 == 0:
                    pe.wait_ge(p1_x[k // 2], i * 16 + 16)
                wait(pe, p1_relu, g - 1)
                nc.tensor.matmul(pa[0:M1, k % 2, :], we_stack[:, :], xs[:, k // 2, k % 2 * GROUP:(k % 2 + 1) * GROUP],
                                 start=True, stop=True).then_inc(p1_lin, 1)

            for k in range(8):
                p1_group(k, k, 0)
            with pe.Fori(1, NG // 8) as i:
                for k in range(8):
                    p1_group(i * 8 + k, k, i)
            for k in range(NG % 8):
                p1_group(NG // 8 * 8 + k, k, NG // 8)
            pe.wait_ge(shift_ready, 1)
            nc.tensor.matmul(pd[0:M1, 0, 0:C], t_col[:, :], w3[:, :], start=True, stop=True).then_inc(shift_made, 1)

            pe.wait_ge(flag_ready, 1)
            outside = pe.value_load(flag[0:1, 0:1], min_val=0, max_val=2 * P)
            pe.wait_ge(main_ready, 1)
            with pe.If(outside < 1):
                def edges(i, j):
                    i, j = at(i, j)
                    if not exists(i, j):
                        return
                    g, n = num(i, j), tiles(i, j)
                    if j % 2 == 0:
                        pe.wait_ge(x_main[j // 2], i * 16 + 16)
                    wait(pe, edge_relu, g - 1)
                    nc.tensor.matmul(pa[0:M1, j % 2, 0:n * TILE], we_stack[:, :],
                                     xs[:, j // 2, j % 2 * GROUP:j % 2 * GROUP + n * TILE],
                                     start=True, stop=True).then_inc(edge_lin, 1)
                    pe.wait_ge(hot_built, g + 1)
                    wait(pe, hot_kept, g - 1)
                    for t in range(n):
                        last = nc.tensor.transpose(pb[0:WIN, j % 2, t * TILE:(t + 1) * TILE], hot[:, j, t, :],
                                                   ident[:, :])
                    last.then_inc(hot_turned, 1)

                def products(i, j):
                    i, j = at(i, j)
                    if not exists(i, j):
                        return
                    g, n = num(i, j), tiles(i, j)
                    pe.wait_ge(edge_relu, g + 1)
                    pe.wait_ge(hot_kept, g + 1)
                    pe.wait_ge(q_in[j], i * 16 + 16)
                    wait(pe, msg_relu, g - 1)
                    for t in range(n):
                        out = pc[:, j % 2, t * C:(t + 1) * C]
                        nc.tensor.matmul(out, r_sb[:, j % 2, t * TILE:(t + 1) * TILE], w3c[:, :],
                                         start=True, stop=False)
                        last = nc.tensor.matmul(out, hot_n[:, j % 2, t * TILE:(t + 1) * TILE], q_win[:, j, :],
                                                start=False, stop=True)
                    last.then_inc(pre_summed, 1)

                def window_sum(i, j):
                    g, n = num(i, j), tiles(i, j)
                    pe.wait_ge(msg_relu, g + 1)
                    wait(pe, win_added, g - 1)
                    for t in range(n):
                        last = nc.tensor.matmul(pd[0:M1, j % 2, 0:WIN], msg[:, j % 2, t, 0:M1], hot[:, j, t, :],
                                                start=(t == 0), stop=(t == n - 1))
                    last.then_inc(win_summed, 1)

                edges(0, 0)
                edges(0, 1)
                products(0, 0)

                def fast(i):
                    for j in range(BODY):
                        edges(i, j + 2)
                        products(i, j + 1)
                        window_sum(i, j)
                passes(pe, fast)
            with pe.Else():
                with pe.Fori(0, NG) as g:
                    pe.wait_ge(gen_turn, g + 1)
                    pe.wait_ge(gen_x, g * 16 + 16)
                    nc.tensor.matmul(pa[0:M1, 0, :], we_stack[:, :], xs[:, 0, 0:GROUP],
                                     start=True, stop=True).then_inc(gen_lin, 1)
                    pe.wait_ge(gen_relu, g + 1)
                    for t in range(TPG):
                        last = nc.tensor.matmul(pc[:, 0, t * C:(t + 1) * C], r_sb[:, 0, t * TILE:(t + 1) * TILE],
                                                w3c[:, :], start=True, stop=True)
                    last.then_inc(gen_sum, 1)
                    with pe.Fori(0, GEN_WINS) as w:
                        pe.wait_ge(gen_msg, g + 1)
                        pe.wait_ge(gen_hot, g * GEN_WINS + w + 1)
                        for t in range(TPG):
                            last = nc.tensor.matmul(pd[0:M1, 0, 0:WIN], msg[:, 0, t, 0:M1], hot[:, 0, t, :],
                                                    start=(t == 0), stop=(t == TPG - 1))
                        last.then_inc(gen_win, 1)

            pe.wait_ge(messages_done, 1)
            for k, lo in ((0, 0), (1, M1)):
                for t in range(TPG):
                    last = nc.tensor.matmul(pd[0:C, 0, k:k + 1], acc[:, t, lo:lo + C], ones[:, :],
                                            start=(t == 0), stop=(t == TPG - 1))
            last.then_inc(sums_made, 1)
            pe.wait_ge(fold_ready, 1)
            nc.tensor.transpose(pa[0:M1, 0, 0:C], fold[:, :], ident[0:C, 0:C]).then_inc(fold_turned, 1)
            pe.wait_ge(diag_kept, 1)
            for q in range(NQ):
                wait(pe, out_ready, q - 1)
                nc.tensor.matmul(pc[0:C, q % 2, 0:nodes(q)], s_diag[:, :], agg[:, 512 * q:512 * q + nodes(q)],
                                 start=True, stop=True).then_inc(out_made, 1)

        @block.vector
        def _(dve):
            steps = [0]

            def link(ins):
                steps[0] += 1
                ins.then_inc(dve_step, 1)
                dve.wait_ge(dve_step, steps[0])

            V = nc.vector
            dve.sem_inc(pre_added, RING)
            V.memset(we5[:, :], 0.0)
            link(V.memset(ones[:, :], 1.0))
            V.memset(we5[0:1, C:M1], 1.0).then_inc(zeroed, 1)
            V.memset(t_col[:, :], 0.0)
            V.memset(bad[:, :], 0.0)
            V.memset(acc[:, :, :], 0.0)

            def ln_stats(c):
                dve.wait_ge(x_in[c], 16)
                b0, b1 = c * LN_CHUNK, (c + 1) * LN_CHUNK
                for b in range(b0, b1):
                    last = V.bn_stats(ln_st[:, b, :], zn[:, b, :])
                link(last)
                st, w = ln_st[:, b0:b1, :], ln_w[:, :, b0:b1]
                V.tensor_tensor(w[:, 4, :], st[:, :, 1], st[:, :, 4], ALU.add)
                V.tensor_tensor(w[:, 1, :], st[:, :, 2], st[:, :, 5], ALU.add)
                link(V.tensor_tensor(w[:, 0, :], st[:, :, 1], st[:, :, 4], ALU.subtract))
                link(V.tensor_tensor(w[:, 0, :], w[:, 0, :], w[:, 0, :], ALU.mult))
                link(V.scalar_tensor_tensor(w[:, 1, :], w[:, 0, :], C / 4.0, w[:, 1, :], ALU.mult, ALU.add))
                V.tensor_scalar(w[:, 2, :], w[:, 1, :], 1.0 / C, EPS, ALU.mult, ALU.add).then_inc(ln_var, 1)
                V.tensor_scalar(w[:, 4, :], w[:, 4, :], 0.5, None, ALU.mult)

            def ln_apply(c):
                b0, b1 = c * LN_CHUNK, (c + 1) * LN_CHUNK
                dve.wait_ge(ln_sqrt, c + 1)
                link(V.reciprocal(ln_rstd[:, b0:b1], ln_rstd[:, b0:b1]))
                for b in range(b0, b1):
                    last = V.tensor_scalar(zn[:, b, :], zn[:, b, :], ln_mean[:, b:b + 1], ln_rstd[:, b:b + 1],
                                           ALU.subtract, ALU.mult)
                last.then_inc(z_ready, 1)

            chunks = NB // LN_CHUNK
            ln_stats(0)
            for c in range(chunks):
                if c + 1 < chunks:
                    ln_stats(c + 1)
                ln_apply(c)

            dve.wait_ge(consts_in, N_CONSTS)
            link(V.tensor_copy(we_split[:, 0, :], we5[:, :]))
            link(V.tensor_tensor(we5[:, :], we5[:, :], we_split[:, 0, :], ALU.subtract))
            link(V.tensor_copy(we_split[:, 1, :], we5[:, :]))
            link(V.tensor_tensor(we5[:, :], we5[:, :], we_split[:, 1, :], ALU.subtract))
            V.tensor_copy(we_split[:, 2, :], we5[:, :]).then_inc(we_ready, 1)

            dve.wait_ge(dst_in, 32)
            rel = dst_rel[:, :, :].rearrange("p g t -> p (g t)")
            far = msg[:, :, :, :].rearrange("p a t w -> p (a t w)")[:, 0:NTILES]
            link(V.tensor_tensor(dst_rel[:, :, :], dst_i[:, 0:NTILES].rearrange("p (g t) -> p g t", t=TPG),
                                 base_b[:, :].unsqueeze(2).to_broadcast([P, NG, TPG]), ALU.subtract))
            full = (NG - 1) * TPG + LAST_TILES - 1
            link(V.tensor_scalar(far, rel, -(WIN - 1) / 2.0, None, ALU.add))
            link(V.tensor_tensor(far, far, far, ALU.mult))
            V.tensor_reduce(bad[:, 0:1], far[:, 0:full], AX, ALU.max)
            link(V.tensor_copy(bad[0:LAST_ROWS, 1:2], far[0:LAST_ROWS, full:full + 1]))
            V.tensor_scalar(bad[:, 2:4], bad[:, 0:2], (WIN / 2.0) ** 2, None, ALU.is_gt).then_inc(bad_ready, 1)
            for k in range(2):
                V.memset(msg[:, k, :, C:M1], 1.0)

            for q in range(NQ):
                dve.wait_ge(p_made, q + 1)
                V.tensor_copy(zn[:, 4 * q:4 * q + quad(q), :].rearrange("p b c -> p (b c)"),
                              pc[:, q % 2, 0:C * quad(q)]).then_inc(p_kept, 1)
            dve.wait_ge(bad_counted, 1)
            V.tensor_reduce(flag[0:1, 0:1], pd[0:1, 0, 0:2], AX, ALU.max).then_inc(flag_ready, 1)
            for q in range(NQ):
                dve.wait_ge(node_relu, q + 1)
                last = V.bn_stats(node_st[:, q, :], node_t[:, 512 * q:512 * q + nodes(q)])
            link(last)
            link(V.bn_aggr(sc[:, 6:8], node_st[:, :, :].rearrange("c q s -> c (q s)")))

            def p1_group(g, k, n):
                dve.wait_ge(p1_relu, g + 1)
                return V.bn_stats(edge_st[:, bass.ds(g, 1), :].rearrange("c a s -> c (a s)"),
                                  r_sb[0:C, k % 2, 0:n]).then_inc(p1_stat, 1)

            with dve.Fori(0, NG // 8) as i:
                for k in range(8):
                    p1_group(i * 8 + k, k, GROUP)
            for k in range(NG % 8):
                g = NG // 8 * 8 + k
                p1_group(g, k, LAST_EDGES if g == NG - 1 else GROUP)
            dve.wait_ge(p1_stat, NG)
            link(V.bn_aggr(sc[:, 0:2], edge_st[:, :, :].rearrange("c g s -> c (g s)")))
            V.tensor_scalar(sc[:, 2:3], sc[:, 1:2], EPS, None, ALU.add)
            V.tensor_scalar(sc[:, 3:4], sc[:, 7:8], EPS, None, ALU.add).then_inc(sqrt_asked, 1)
            dve.wait_ge(sqrt_done, 1)
            link(V.reciprocal(sc[:, 4:6], sc[:, 4:6]))
            V.tensor_tensor(sc[:, 8:9], sc[:, 4:5], vec[:, G_EDGE:G_EDGE + 1], ALU.mult)
            link(V.tensor_tensor(sc[:, 10:11], sc[:, 5:6], vec[:, G_NODE:G_NODE + 1], ALU.mult))
            V.tensor_scalar(w3c[0:C, :], w3[:, :], sc[:, 8:9], None, ALU.mult)
            V.tensor_tensor(sc[:, 9:10], sc[:, 0:1], sc[:, 8:9], ALU.mult)
            link(V.tensor_tensor(sc[:, 13:14], sc[:, 6:7], sc[:, 10:11], ALU.mult))
            V.tensor_tensor(t_col[:, C:M1], vec[:, BT_EDGE:BT_EDGE + 1], sc[:, 9:10],
                            ALU.subtract).then_inc(shift_ready, 1)
            dve.wait_ge(node_made, NQ)
            link(V.memset(agg, 0.0))
            dve.wait_ge(shift_made, 1)
            V.tensor_tensor(w3c[C:M1, :], pd[C:M1, 0, 0:C], bm_row[C:M1, :], ALU.add).then_inc(main_ready, 1)

            outside = dve.value_load(flag[0:1, 0:1], min_val=0, max_val=2 * P)
            with dve.If(outside < 1):
                def build_hot(i, j):
                    i, j = at(i, j)
                    if not exists(i, j):
                        return
                    g, n = num(i, j), tiles(i, j)
                    wait(dve, win_summed, g - 3)
                    V.tensor_tensor(hot[:, j, 0:n, :],
                                    dst_rel[:, bass.ds(g, 1), 0:n].rearrange("p a t -> p (a t)").unsqueeze(2).to_broadcast([P, n, WIN]),
                                    ramp[:, :].unsqueeze(1).to_broadcast([P, n, WIN]),
                                    ALU.is_equal).then_inc(hot_built, 1)

                def add_gathered(i, j):
                    i, j = at(i, j)
                    if not exists(i, j):
                        return
                    g, n = num(i, j), tiles(i, j) * C
                    dve.wait_ge(pre_summed, g + 1)
                    dve.wait_ge(gathered, g + 1)
                    V.tensor_tensor(pc[:, j % 2, 0:n], pc[:, j % 2, 0:n],
                                    ring[:, bass.ds((g % RING) * (TPG * C), n)], ALU.add).then_inc(pre_added, 1)

                def add_sums(i, j):
                    g, n = num(i, j), tiles(i, j)
                    base = dve.value_load(base_b[0:1, bass.ds(g, 1)], min_val=0, max_val=N - 1)
                    dve.wait_ge(msg_square, g + 1)
                    wait(dve, acc_added, g)
                    V.tensor_tensor(acc[:, 0:n, :], acc[:, 0:n, :], msg[:, j % 2, 0:n, :],
                                    ALU.add).then_inc(acc_added, 1)
                    dve.wait_ge(win_summed, g + 1)
                    wait(dve, win_added, g)
                    V.tensor_tensor(agg[:, bass.ds(base, WIN)], agg[:, bass.ds(base, WIN)], pd[0:M1, j % 2, 0:WIN],
                                    ALU.add).then_inc(win_added, 1)

                for j in range(3):
                    build_hot(0, j)
                add_gathered(0, 0)

                def fast(i):
                    for j in range(BODY):
                        build_hot(i, j + 3)
                        add_gathered(i, j + 1)
                        add_sums(i, j)
                passes(dve, fast)
                dve.wait_ge(acc_added, NG)
                dve.wait_ge(win_added, NG)
            with dve.Else():
                dve.sem_inc(gen_turn, 1)
                far4 = bad[:, 0:TPG]
                with dve.Fori(0, NG) as g:
                    dve.wait_ge(gen_dst, g * 16 + 16)
                    V.tensor_copy(far4, dst_i2[:, 0:TPG]).then_inc(gen_step, 1)
                    dve.wait_ge(gen_sum, g + 1)
                    dve.wait_ge(gen_rows, g * (32 * TPG) + 32 * TPG)
                    per = GEN_WINS * 2 + 3
                    V.tensor_tensor(pc[:, 0, 0:TPG * C], pc[:, 0, 0:TPG * C], ring[:, 0:TPG * C],
                                    ALU.add).then_inc(gen_step, 1)
                    dve.wait_ge(gen_step, g * per + 2)
                    V.tensor_tensor(pc[:, 0, 0:TPG * C], pc[:, 0, 0:TPG * C], ring[:, TPG * C:2 * TPG * C],
                                    ALU.add).then_inc(gen_pre, 1)
                    dve.wait_ge(gen_square, g + 1)
                    V.tensor_tensor(acc[:, :, :], acc[:, :, :], msg[:, 0, :, :], ALU.add).then_inc(gen_step, 1)
                    with dve.Fori(0, GEN_WINS) as w:
                        V.tensor_tensor(hot[:, 0, :, :], far4.unsqueeze(2).to_broadcast([P, TPG, WIN]),
                                        ramp[:, :].unsqueeze(1).to_broadcast([P, TPG, WIN]),
                                        ALU.is_equal).then_inc(gen_hot, 1)
                        dve.wait_ge(gen_win, g * GEN_WINS + w + 1)
                        V.tensor_scalar(far4, far4, -float(WIN), None, ALU.add).then_inc(gen_step, 1)
                        V.tensor_tensor(agg[:, bass.ds(w * WIN, WIN)], agg[:, bass.ds(w * WIN, WIN)],
                                        pd[0:M1, 0, 0:WIN], ALU.add).then_inc(gen_step, 1)
                        dve.wait_ge(gen_step, g * per + w * 2 + 5)
                    V.memset(flag[0:1, 0:1], 0).then_inc(gen_turn, 1)
                dve.wait_ge(gen_turn, NG + 1)

            V.memset(fold[:, :], 0.0).then_inc(messages_done, 1)
            dve.wait_ge(res_in, 16)
            link(V.tensor_tensor(sc[:, 14:15], vec[:, BT_NODE:BT_NODE + 1], sc[:, 13:14], ALU.subtract))
            link(V.tensor_scalar(node_t, node_t, sc[:, 10:11], sc[:, 14:15], ALU.mult, ALU.add))
            link(V.tensor_tensor(node_t, node_t, res_t, ALU.add))
            dve.wait_ge(sums_made, 1)
            link(V.tensor_scalar(sc[:, 0:2], pd[0:C, 0, 0:2], 1.0 / E, None, ALU.mult))
            link(V.tensor_tensor(sc[:, 2:3], sc[:, 0:1], sc[:, 0:1], ALU.mult))
            link(V.tensor_tensor(sc[:, 3:4], sc[:, 1:2], sc[:, 2:3], ALU.subtract))
            V.tensor_scalar(sc[:, 11:12], sc[:, 3:4], 0.0, EPS, ALU.max, ALU.add).then_inc(sqrt_asked, 1)
            dve.wait_ge(sqrt_done, 2)
            link(V.reciprocal(sc[:, 12:13], sc[:, 12:13]))
            link(V.tensor_tensor(sc[:, 8:9], sc[:, 12:13], vec[:, G_MSG:G_MSG + 1], ALU.mult))
            V.tensor_scalar(fold[:, 0:C], ident[0:C, 0:C], sc[:, 8:9], None, ALU.mult)
            link(V.tensor_tensor(sc[:, 9:10], sc[:, 0:1], sc[:, 8:9], ALU.mult))
            V.tensor_tensor(fold[:, C:M1], vec[:, BT_MSG:BT_MSG + 1], sc[:, 9:10],
                            ALU.subtract).then_inc(fold_ready, 1)
            dve.wait_ge(fold_turned, 1)
            V.tensor_copy(s_diag[:, :], pa[0:M1, 0, 0:C]).then_inc(diag_kept, 1)
            for q in range(NQ):
                dve.wait_ge(out_made, q + 1)
                part = node_t[:, 512 * q:512 * q + nodes(q)]
                V.tensor_tensor(part, part, pc[0:C, q % 2, 0:nodes(q)], ALU.add).then_inc(out_ready, 1)


def kernel(**inputs):
    import numpy as _np
    import concourse.bacc as _bacc
    from concourse import mybir as _mybir
    from concourse.bass_utils import run_bass_kernel_spmd as _run

    x, src, dst, ea = (_np.asarray(inputs[k]) for k in ("x", "src", "dst", "edge_attr_4"))
    w = {k[7:]: _np.asarray(v) for k, v in inputs.items() if k.startswith("L0_gnn_")}
    x_pad = _np.zeros((NP, C), x.dtype)
    x_pad[:N] = x
    src_pad = _np.full(IDX_W * TILE, N, src.dtype)
    src_pad[:E] = src
    dst_pad = _np.full(EP, N, dst.dtype)
    dst_pad[:E] = dst
    rows = _np.zeros((EROWS, EP), ea.dtype)
    rows[0, :E] = 1.0
    rows[1:, :E] = ea.T
    arrays = {
        "x_nodes": x_pad.reshape(NB, P, C).transpose(1, 0, 2),
        "x_t": x.T,
        "src_cols": src_pad.reshape(IDX_W, TILE).T,
        "dst_cols": dst_pad.reshape(NTILES, TILE).T,
        "group_base": dst_pad[::GROUP],
        "edge_rows": rows.reshape(P, SPLIT_F),
        "w_node": w["W_node"], "b_node": w["b_node"][:, None], "g_node": w["g_node"][:, None],
        "beta_node": w["beta_node"][:, None],
        "w_edge": w["W_edge"], "b_edge": w["b_edge"][None, :], "g_edge": w["g_edge"][:, None],
        "beta_edge": w["beta_edge"][:, None],
        "w_msg": w["W_msg"], "b_msg": w["b_msg"][None, :], "g_msg": w["g_msg"][:, None],
        "beta_msg": w["beta_msg"][:, None],
        "ident": _np.eye(P, dtype=_np.float32),
        "ramp": _np.tile(_np.arange(WIN, dtype=_np.float32), (P, 1)),
    }
    nc = _bacc.Bacc("TRN2", target_bir_lowering=False, num_devices=1)
    args = []
    for name in list(arrays):
        a = arrays["in_" + name] = _np.ascontiguousarray(arrays.pop(name))
        args.append(nc.dram_tensor("in_" + name, a.shape, _mybir.dt.from_np(a.dtype), kind="ExternalInput").ap())
    args.append(nc.dram_tensor("out_t", (C, N), _mybir.dt.float32, kind="ExternalOutput").ap())
    graph_layer(nc, *args)
    r = _run(nc, [arrays], core_ids=[0])
    return _np.ascontiguousarray(r.results[0]["out_t"].T)
```

```python
import concourse.bass as bass
from concourse import mybir
from contextlib import ExitStack

N, E, C, EF = 6250, 100000, 96, 4
P = 128
TILE = P
TPG = 4
GROUP = TPG * TILE
NG = -(-E // GROUP)
NTILES = NG * TPG
LAST_EDGES = E - (NG - 1) * GROUP
LAST_TILES = -(-LAST_EDGES // TILE)
LAST_ROWS = LAST_EDGES - (LAST_TILES - 1) * TILE
EP = NG * GROUP
WIN = 96
NB = -(-(N + WIN) // P)
NP = NB * P
NQ = -(-NB // 4)
EPS = 1e-5
STACK = (("hi", "hi"), ("hi", "mid"), ("hi", "lo"), ("mid", "hi"), ("mid", "mid"), ("lo", "hi"))
EROWS = EF + 1
KROWS = len(STACK) * EROWS
SPLIT_F = EROWS * EP // P
BODY = 4
LOOPS = NG // BODY
RAW = 8
RING = 60
ROUNDS = (NG - RAW) // RING
AHEAD = 3
HALF = RING // 2 * TPG
IDX_W = (RAW + AHEAD + ROUNDS * RING) * TPG + HALF
LN_CHUNK = 10
RAW_CHUNK = 2
NODE_CHUNK = -(-N // LOOPS)
GEN_WINS = -(-N // WIN)
M1 = C + 1
RAMP_AT = P
WN_AT = RAMP_AT + WIN
BM_AT = WN_AT + 4 * C
VEC_AT = BM_AT + C
PACKED = VEC_AT + 7
P1_LOOPS = NG // 8
P1_TAIL = NG % 8 // 2
P1_PEELED = 3
MLP_CHUNK = N // (P1_LOOPS + 1)
MW = C + 1 + C


def graph_layer(nc, x_rows, x_nodes, x_t, src_cols, dst_cols, group_base, edge_rows, packed, w_edge, out_t):
    fp32, bf16, i32 = mybir.dt.float32, mybir.dt.bfloat16, mybir.dt.int32
    ALU, ACT, AX = mybir.AluOpType, mybir.ActivationFunctionType, mybir.AxisListType.X

    p_table = nc.dram_tensor("p_table", (NP, C), fp32, kind="Internal").ap()
    q_table = nc.dram_tensor("q_table", (NP, C), fp32, kind="Internal").ap()
    x_stack = nc.dram_tensor("x_stack", (KROWS, EP), bf16, kind="Internal").ap()

    with ExitStack() as ctx:
        def sb(name, shape, dt=fp32):
            return ctx.enter_context(nc.sbuf_tensor(name, shape, dt))

        def sem(name):
            return ctx.enter_context(nc.semaphore(name))

        ring = sb("ring", [P, RING * TPG * C])
        splits_at = RING * TPG * C - -(-3 * SPLIT_F // 2)
        node_at = splits_at - NB * C
        splits_slot, node_slot = splits_at // (TPG * C), node_at // (TPG * C)
        zn = ring[:, node_at:splits_at].rearrange("p (b c) -> p b c", c=C)
        raw = ring[:, 0:RAW * TPG * C].rearrange("p (b c) -> p b c", c=C)
        splits = ring[:, splits_at:splits_at + 3 * SPLIT_F // 2].bitcast(bf16).rearrange("p (s f) -> p s f", s=3)
        big_a = sb("big_a", [P, NP])
        h_t, agg = big_a[0:C, :], big_a[0:M1, :]
        big_b = sb("big_b", [P, N])
        node_t, edge_f = big_b[0:C, :], big_b[:, 0:SPLIT_F]
        res = sb("res", [C, NODE_CHUNK])
        xs = sb("xs", [KROWS, 4, 2 * GROUP], bf16)
        src_i = sb("src_i", [P, IDX_W], i32)
        idx_buf = sb("idx_buf", [P, 2, HALF], i32)
        dst_rel = sb("dst_rel", [P, NG, TPG])
        base_b = sb("base_b", [P, NG], i32)
        hot = sb("hot", [P, 4, TPG, WIN])
        dst_i = hot[:, :, :, :].bitcast(i32).rearrange("p a t w -> p (a t w)")
        dst_i2 = hot[:, 2:4, :, :].bitcast(i32).rearrange("p a t w -> p (a t w)")
        r_sb = sb("r_sb", [M1, 2, 2 * GROUP])
        hot_n = sb("hot_n", [WIN, 2, GROUP])
        msg = sb("msg", [P, 2, TPG, MW])
        acc = sb("acc", [P, TPG, MW])
        edge_st = sb("edge_st", [C, NG, 6])
        node_st = sb("node_st", [C, P1_LOOPS + 1, 6])
        ln_st = sb("ln_st", [P, NB + RAW * TPG, 6])
        ln_w = sb("ln_w", [P, 6, NB + RAW * TPG])
        q_win = sb("q_win", [WIN, 4, C])
        ones = sb("ones", [P, 1])
        pk = sb("pk", [P, PACKED])
        ident, ramp = pk[:, 0:P], pk[:, RAMP_AT:RAMP_AT + WIN]
        wn, w1, w2, w3 = (pk[0:C, WN_AT + k * C:WN_AT + (k + 1) * C] for k in range(4))
        bm_row, vec = pk[0:M1, BM_AT:BM_AT + C], pk[0:C, VEC_AT:VEC_AT + 7]
        w3c = sb("w3c", [M1, C])
        we5 = sb("we5", [EROWS, M1])
        we_split = sb("we_split", [EROWS, 3, M1], bf16)
        we_stack = sb("we_stack", [KROWS, M1], bf16)
        sc = sb("sc", [C, 16])
        t_col = sb("t_col", [C, M1])
        fold = sb("fold", [C, M1])
        s_diag = sb("s_diag", [M1, C])
        bad = sb("bad", [P, 4])
        flag = sb("flag", [1, 1], i32)
        ln_rstd, ln_mean, ln_shift = ln_w[:, 3, :], ln_w[:, 4, :], ln_w[:, 5, :]

        pa = ctx.enter_context(nc.psum_tensor("pa", [P, 2, 512], fp32))
        pb = ctx.enter_context(nc.psum_tensor("pb", [P, 2, 512], fp32))
        pc = ctx.enter_context(nc.psum_tensor("pc", [P, 2, 512], fp32))
        pd = ctx.enter_context(nc.psum_tensor("pd", [P, 2, 512], fp32))

        B_NODE, G_NODE, BT_NODE, G_EDGE, BT_EDGE, G_MSG, BT_MSG = range(7)

        x_in = [sem(f"x_in{c}") for c in range(NB // LN_CHUNK)]
        edge_in = sem("edge_in")
        consts_in = sem("consts_in")
        we_in = sem("we_in")
        dst_in = sem("dst_in")
        src_in = sem("src_in")
        zeroed = sem("zeroed")
        dve_step = sem("dve_step")
        ln_var = sem("ln_var")
        ln_sqrt = sem("ln_sqrt")
        z_ready = sem("z_ready")
        z_turned = sem("z_turned")
        z_scales = sem("z_scales")
        z_by_act = sem("z_by_act")
        h_kept = sem("h_kept")
        p_made = sem("p_made")
        p_kept = sem("p_kept")
        p_stored = sem("p_stored")
        q_made = sem("q_made")
        q_kept = sem("q_kept")
        q_stored = sem("q_stored")
        node_made = sem("node_made")
        node_relu = sem("node_relu")
        node_stat = sem("node_stat")
        split_step = sem("split_step")
        raw_done = [sem(f"raw_done{k}") for k in range(RAW // RAW_CHUNK)]
        agg_zeroed = sem("agg_zeroed")
        stack_stored = sem("stack_stored")
        we_ready = sem("we_ready")
        we_placed = sem("we_placed")
        bad_ready = sem("bad_ready")
        bad_counted = sem("bad_counted")
        flag_ready = sem("flag_ready")
        res_in = sem("res_in")
        sqrt_asked = sem("sqrt_asked")
        sqrt_done = sem("sqrt_done")
        shift_ready = sem("shift_ready")
        shift_made = sem("shift_made")
        p1_x = [sem(f"p1_x{k}") for k in range(4)]
        p1_lin = sem("p1_lin")
        p1_relu = sem("p1_relu")
        p1_stat = sem("p1_stat")
        main_ready = sem("main_ready")
        idx_ready = sem("idx_ready")
        gather_done = [sem(f"gather_done{k}") for k in range(4)]
        gathered = sem("gathered")
        x_main = [sem(f"x_main{k}") for k in range(2)]
        q_in = [sem(f"q_in{k}") for k in range(4)]
        edge_lin = sem("edge_lin")
        edge_relu = sem("edge_relu")
        hot_built = sem("hot_built")
        hot_turned = sem("hot_turned")
        hot_kept = sem("hot_kept")
        pre_summed = sem("pre_summed")
        pre_added = sem("pre_added")
        msg_relu = sem("msg_relu")
        msg_square = sem("msg_square")
        win_summed = sem("win_summed")
        win_added = sem("win_added")
        acc_added = sem("acc_added")
        node_added = sem("node_added")
        gen_turn = sem("gen_turn")
        gen_x = sem("gen_x")
        gen_idx = sem("gen_idx")
        gen_rows = sem("gen_rows")
        gen_claimed = sem("gen_claimed")
        gen_lin = sem("gen_lin")
        gen_relu = sem("gen_relu")
        gen_sum = sem("gen_sum")
        gen_dst = sem("gen_dst")
        gen_pre = sem("gen_pre")
        gen_msg = sem("gen_msg")
        gen_square = sem("gen_square")
        gen_hot = sem("gen_hot")
        gen_win = sem("gen_win")
        gen_step = sem("gen_step")
        messages_done = sem("messages_done")
        sums_made = sem("sums_made")
        fold_ready = sem("fold_ready")
        fold_turned = sem("fold_turned")
        diag_kept = sem("diag_kept")
        out_made = sem("out_made")
        out_ready = sem("out_ready")
        out_stored = sem("out_stored")

        def at(i, j):
            return i + j // BODY, j % BODY

        def num(i, j):
            return i * BODY + j

        def exists(i, j):
            return not isinstance(i, int) or 0 <= num(i, j) < NG

        def wait(eng, s, value):
            if not isinstance(value, int) or value > 0:
                eng.wait_ge(s, value)

        def tiles(i, j):
            return LAST_TILES if isinstance(i, int) and num(i, j) == NG - 1 else TPG

        def passes(eng, body):
            body(0)
            with eng.Fori(1, LOOPS - 1) as i:
                body(i)
            body(LOOPS - 1)

        assert MLP_CHUNK * (P1_LOOPS + 1) == N and NQ <= 4 * P1_PEELED + 1

        def p1_passes(eng, body, tail):
            for i in range(P1_PEELED):
                body(i)
            with eng.Fori(P1_PEELED, P1_LOOPS) as i:
                body(i)
            tail(P1_LOOPS)

        def p1_quads(i, k):
            if not isinstance(i, int) or i >= P1_PEELED:
                return []
            u = 4 * i + k
            return [q for q in (u, u + 1) if q < NQ and (q == u or u == 4 * P1_PEELED - 1)]

        def node_cols(i):
            return min(NODE_CHUNK, N - i * NODE_CHUNK) if isinstance(i, int) else NODE_CHUNK

        def quad(q):
            return min(4, NB - 4 * q) if q < NQ else TPG

        def rows_of(q):
            return zn[:, 4 * q:4 * q + quad(q), :] if q < NQ else raw[:, (q - NQ) * TPG:(q - NQ + 1) * TPG, :]

        def h_of(q):
            return h_t[:, 512 * q:512 * q + 128 * quad(q)] if q < NQ else r_sb[0:C, q % 2, 0:GROUP]

        N_LN = NB // LN_CHUNK
        N_RAW = RAW // RAW_CHUNK

        def ln_blocks(c):
            if c < N_LN:
                return zn[:, c * LN_CHUNK:(c + 1) * LN_CHUNK, :], c * LN_CHUNK, LN_CHUNK
            k = (c - N_LN) * RAW_CHUNK * TPG
            return raw[:, k:k + RAW_CHUNK * TPG, :], NB + k, RAW_CHUNK * TPG

        def ln_quads(c):
            if c >= N_LN:
                return range(NQ + (c - N_LN) * RAW_CHUNK, NQ + (c - N_LN + 1) * RAW_CHUNK)
            return [q for q in range(NQ) if c * LN_CHUNK < 4 * q + quad(q) <= (c + 1) * LN_CHUNK]

        def ln_by_act(c):
            return LN_CHUNK // 2 if c < N_LN else 0

        def nodes(q):
            return min(512, N - 512 * q)

        block = ctx.enter_context(nc.Block())

        @block.sync
        def _(sp):
            def stack_rows(k):
                rows = x_stack[k * EROWS:(k + 1) * EROWS, :].rearrange("r e -> (r e)")
                return rows.rearrange("(p f) -> p f", p=P)

            for c in range(NB // LN_CHUNK):
                b0 = c * LN_CHUNK
                sp.dma_start(zn[:, b0:b0 + LN_CHUNK, :], x_nodes[:, b0:b0 + LN_CHUNK, :]).then_inc(x_in[c], 16)
            sp.dma_start(edge_f, edge_rows).then_inc(edge_in, 16)
            for q in range(NQ):
                sp.wait_ge(p_kept, q + 1)
                sp.dma_start(p_table[512 * q:512 * q + 128 * quad(q), :].rearrange("(b p) c -> p b c", p=P),
                             zn[:, 4 * q:4 * q + quad(q), :]).then_inc(p_stored, 16)
            for s, name in enumerate(("hi", "mid", "lo")):
                sp.wait_ge(split_step, 2 * s + 1)
                for k, (part, _) in enumerate(STACK):
                    if part == name:
                        sp.dma_start(stack_rows(k), splits[:, s, :]).then_inc(stack_stored, 16)
            sp.wait_ge(stack_stored, 16 * len(STACK))

            def load_p1(i, units=4):
                for k in range(units):
                    u = i * 4 + k
                    wait(sp, p1_lin, u - 3)
                    sp.dma_start(xs[:, k, :], x_stack[:, bass.ts(u, 2 * GROUP)]).then_inc(p1_x[k], 16)
                if isinstance(i, int) and 0 < i <= P1_PEELED:
                    for q in [q for j in range(4) for q in p1_quads(i - 1, j)]:
                        sp.wait_ge(q_kept, q + 1)
                        sp.dma_start(q_table[512 * q:512 * q + 128 * quad(q), :].rearrange("(b p) c -> p b c", p=P),
                                     rows_of(q)).then_inc(q_stored, 16)

            for i in range(P1_PEELED + 1):
                load_p1(i)
            with sp.Fori(P1_PEELED + 1, P1_LOOPS) as i:
                load_p1(i)
            load_p1(P1_LOOPS, P1_TAIL)
            sp.wait_ge(node_made, P1_LOOPS + 1)
            sp.wait_ge(zeroed, 1)
            sp.dma_start(agg.rearrange("c (a b) -> c a b", b=NP // 10),
                         acc[0:M1, :, :].rearrange("c t m -> c (t m)")[:, 0:NP // 10].unsqueeze(1).to_broadcast(
                             [M1, 10, NP // 10])).then_inc(agg_zeroed, 16)

            def load_res(i):
                wait(sp, node_added, i)
                n = node_cols(i)
                sp.dma_start(res[:, 0:n], x_t[:, bass.ds(i * NODE_CHUNK, n)]).then_inc(res_in, 16)

            sp.wait_ge(p1_lin, NG // 2)
            sp.wait_ge(q_stored, 16 * NQ)
            sp.wait_ge(flag_ready, 1)
            outside = sp.value_load(flag[0:1, 0:1], min_val=0, max_val=2 * P)
            with sp.If(outside < 1):
                def fast(i):
                    for j in range(BODY):
                        g = num(i, j)
                        if j % 2 == 0:
                            wait(sp, edge_lin, g - 2)
                            sp.dma_start(xs[:, j // 2, :], x_stack[:, bass.ds(g * GROUP, 2 * GROUP)]).then_inc(
                                x_main[j // 2], 16)
                        wait(sp, pre_summed, g - 3)
                        base = sp.value_load(base_b[0:1, bass.ds(g, 1)], min_val=0, max_val=N - 1)
                        sp.dma_start(q_win[:, j, :], q_table[bass.ds(base, WIN), :]).then_inc(q_in[j], 16)
                    load_res(i)
                passes(sp, fast)
            with sp.Else():
                with sp.Fori(0, NG) as g:
                    sp.wait_ge(gen_turn, g + 1)
                    sp.dma_start(xs[:, 0, 0:GROUP], x_stack[:, bass.ds(g * GROUP, GROUP)]).then_inc(gen_x, 16)
                    sp.dma_start(dst_i2[:, 0:TPG], dst_cols[:, bass.ds(g * TPG, TPG)]).then_inc(gen_dst, 16)
                passes(sp, load_res)

            for q in range(NQ):
                sp.wait_ge(out_ready, q + 1)
                sp.dma_start(out_t[:, 512 * q:512 * q + nodes(q)], node_t[:, 512 * q:512 * q + nodes(q)]).then_inc(
                    out_stored, 16)
            sp.wait_ge(out_stored, 16 * NQ)

        @block.gpsimd
        def _(pool):
            def row_gather(slot, tile, table, idx, done):
                lo = (slot * TPG + tile) * C
                nc.gpsimd.indirect_dma_start(
                    out=ring[:, lo:lo + C], out_offset=None, in_=table,
                    in_offset=bass.IndirectOffsetOnAxis(ap=idx, axis=0)).then_inc(done, 16)

            pool.wait_ge(src_in, 16)
            for g in range(RAW):
                for t in range(TPG):
                    row_gather(g, t, x_rows, src_i[:, g * TPG + t:g * TPG + t + 1], raw_done[g // RAW_CHUNK])
            lo = (RAW + AHEAD) * TPG
            nc.gpsimd.tensor_copy(idx_buf[:, 0, :], src_i[:, lo:lo + HALF]).then_inc(idx_ready, 1)
            pool.sem_inc(gathered, RAW)
            pool.wait_ge(p_stored, 16 * NQ)
            pool.wait_ge(idx_ready, 1)
            pool.wait_ge(flag_ready, 1)
            outside = pool.value_load(flag[0:1, 0:1], min_val=0, max_val=2 * P)
            with pool.If(outside < 1):
                for g in range(RAW, RAW + AHEAD):
                    for t in range(TPG):
                        row_gather(g, t, p_table, src_i[:, g * TPG + t:g * TPG + t + 1], gather_done[g % 4])
                with pool.Fori(0, ROUNDS) as r:
                    for k in range(RING):
                        half, col = k // (RING // 2), k % (RING // 2) * TPG
                        start = RAW + AHEAD + k
                        if start % RING == node_slot:
                            pool.wait_ge(q_stored, 16 * NQ)
                        if start % RING == splits_slot:
                            pool.wait_ge(stack_stored, 16 * len(STACK))
                        for t in range(TPG):
                            row_gather(start % RING, t, p_table, idx_buf[:, half, col + t:col + t + 1],
                                       gather_done[start % 4])
                        pool.wait_ge(gather_done[(RAW + k) % 4], r * (64 * RING // 4) + 64 * (k // 4 + 1))
                        if (k + 1) % (RING // 2) == 0:
                            pool.wait_ge(idx_ready, r * 2 + half + 2)
                        pool.wait_ge(pre_added, r * RING + (start + 2))
                        pool.sem_inc(gathered, 1)
                        if k % (RING // 2) == AHEAD:
                            nc.gpsimd.tensor_copy(
                                idx_buf[:, 1 - half, :],
                                src_i[:, bass.ds(r * (RING * TPG) + (RAW + AHEAD + (half + 1) * (RING // 2)) * TPG, HALF)]
                            ).then_inc(idx_ready, 1)
                for g in range(RAW + ROUNDS * RING, NG):
                    if g + AHEAD < NG:
                        pool.wait_ge(pre_added, g + AHEAD + 1)
                        for t in range(tiles(0, g + AHEAD)):
                            col = (g + AHEAD) * TPG + t
                            row_gather((g + AHEAD) % RING, t, p_table, src_i[:, col:col + 1],
                                       gather_done[(g + AHEAD) % 4])
                    pool.wait_ge(gather_done[g % 4], 64 * ((g - RAW) // 4) + 16 * tiles(0, g))
                    pool.sem_inc(gathered, 1)
            with pool.Else():
                pool.wait_ge(q_stored, 16 * NQ)
                pool.wait_ge(p_kept, NQ + RAW)
                with pool.Fori(0, NG) as g:
                    pool.wait_ge(gen_turn, g + 1)
                    nc.gpsimd.tensor_copy(idx_buf[:, 0, 0:TPG], src_i[:, bass.ds(g * TPG, TPG)]).then_inc(gen_idx, 1)
                    pool.wait_ge(gen_dst, g * 16 + 16)
                    pool.wait_ge(gen_idx, g + 1)
                    pool.sem_inc(gen_claimed, 1)
                    for t in range(TPG):
                        row_gather(0, t, p_table, idx_buf[:, 0, t:t + 1], gen_rows)
                        row_gather(1, t, q_table, dst_i2[:, t:t + 1], gen_rows)

        @block.scalar
        def _(act):
            act.dma_start(src_i[:, :], src_cols).then_inc(src_in, 16)
            act.dma_start(pk[:, :], packed).then_inc(consts_in, 16)
            act.dma_start(we5[:, :], w_edge).then_inc(we_in, 16)
            act.dma_start(dst_i[:, 0:NTILES], dst_cols).then_inc(dst_in, 16)
            act.dma_start(base_b[:, :], group_base.partition_broadcast(P)).then_inc(dst_in, 16)

            def keep_h(q):
                act.wait_ge(z_turned, q + 1)
                nc.scalar.activation(h_of(q), pb[0:C, q % 2, 0:128 * quad(q)], ACT.Relu).then_inc(h_kept, 1)
                if q not in (0, NQ):
                    keep_p(q - 1)

            def keep_p(q):
                act.wait_ge(p_made, q + 1)
                nc.scalar.copy(rows_of(q).rearrange("p b c -> p (b c)"), pc[:, q % 2, 0:C * quad(q)]).then_inc(p_kept, 1)

            def split(s):
                act.wait_ge(split_step, 2 * s) if s else act.wait_ge(edge_in, 16)
                nc.scalar.copy(splits[:, s, :], edge_f).then_inc(split_step, 1)

            def keep_quads(c):
                for q in ln_quads(c):
                    keep_h(q)
                if c in (N_LN - 1, N_LN + N_RAW - 1):
                    keep_p(q)

            for c in range(N_LN + N_RAW):
                rows, b0, n = ln_blocks(c)
                act.wait_ge(ln_var, c + 1)
                nc.scalar.sqrt(ln_w[:, 3, b0:b0 + n], ln_w[:, 2, b0:b0 + n]).then_inc(ln_sqrt, 1)
                if ln_by_act(c):
                    act.wait_ge(z_scales, c + 1)
                    for b in range(ln_by_act(c)):
                        last = nc.scalar.activation(rows[:, b, :], rows[:, b, :], ACT.Identity,
                                                    bias=ln_shift[:, b0 + b:b0 + b + 1],
                                                    scale=ln_rstd[:, b0 + b:b0 + b + 1])
                    last.then_inc(z_by_act, 1)
                if c not in (0, N_LN):
                    keep_quads(c - 1)
                if c == N_LN - 1:
                    keep_quads(c)
                    split(0)
                if c == N_LN + 1:
                    split(1)
                if c == N_LN + 2:
                    split(2)
                if c == N_LN + N_RAW - 1:
                    keep_quads(c)
            act.wait_ge(we_ready, 1)
            for k, (_, part) in enumerate(STACK):
                act.dma_start(we_stack[k * EROWS:(k + 1) * EROWS, :],
                              we_split[:, ("hi", "mid", "lo").index(part), :]).then_inc(we_placed, 16)
            act.wait_ge(p_stored, 16 * NQ)
            act.wait_ge(split_step, 5)

            def p1_unit(i, k):
                u = i * 4 + k
                act.wait_ge(p1_lin, u + 1)
                wait(act, p1_stat, u - 1)
                nc.scalar.activation(r_sb[0:C, k % 2, :], (pa, pb)[k % 2][0:C, :, :].rearrange("c a b -> c (a b)"),
                                     ACT.Relu).then_inc(p1_relu, 1)
                for q in p1_quads(i, k):
                    act.wait_ge(q_made, q + 1)
                    nc.scalar.copy(rows_of(q).rearrange("p b c -> p (b c)"),
                                   pc[:, q % 2, 0:C * quad(q)]).then_inc(q_kept, 1)

            def p1_body(i, units=4):
                for k in range(units):
                    p1_unit(i, k)
                act.wait_ge(node_made, i + 1)
                nc.scalar.activation(node_t[:, bass.ds(i * MLP_CHUNK, MLP_CHUNK)], pd[0:C, 0, 0:MLP_CHUNK], ACT.Relu,
                                     bias=vec[:, B_NODE:B_NODE + 1]).then_inc(node_relu, 1)

            p1_passes(act, p1_body, lambda i: p1_body(i, P1_TAIL))
            act.wait_ge(sqrt_asked, 1)
            nc.scalar.sqrt(sc[:, 4:6], sc[:, 2:4]).then_inc(sqrt_done, 1)

            act.wait_ge(flag_ready, 1)
            outside = act.value_load(flag[0:1, 0:1], min_val=0, max_val=2 * P)
            act.wait_ge(main_ready, 1)
            with act.If(outside < 1):
                def keep_edges(i, j):
                    i, j = at(i, j)
                    if not exists(i, j):
                        return
                    g, n = num(i, j), tiles(i, j) * TILE
                    act.wait_ge(edge_lin, g + 1)
                    wait(act, pre_summed, g - 1)
                    nc.scalar.activation(r_sb[:, j % 2, 0:n], pa[0:M1, j % 2, 0:n], ACT.Relu).then_inc(edge_relu, 1)
                    act.wait_ge(hot_turned, g + 1)
                    nc.scalar.copy(hot_n[:, j % 2, 0:n], pb[0:WIN, j % 2, 0:n]).then_inc(hot_kept, 1)

                def keep_messages(i, j):
                    i, j = at(i, j)
                    if not exists(i, j):
                        return
                    g, n = num(i, j), tiles(i, j)
                    wait(act, win_summed, g - 1)
                    wait(act, acc_added, g - 1)
                    act.wait_ge(pre_added, g + RING + 1)
                    nc.scalar.activation(msg[:, j % 2, 0:n, 0:C],
                                         pc[:, j % 2, 0:n * C].rearrange("p (t c) -> p t c", c=C),
                                         ACT.Relu).then_inc(msg_relu, 1)
                    act.wait_ge(msg_relu, g + 1)
                    nc.scalar.square(msg[:, j % 2, 0:n, M1:MW], msg[:, j % 2, 0:n, 0:C]).then_inc(msg_square, 1)

                keep_edges(0, 0)
                keep_edges(0, 1)
                keep_messages(0, 0)

                def fast(i):
                    for j in range(BODY):
                        keep_edges(i, j + 2)
                        keep_messages(i, j + 1)
                passes(act, fast)
            with act.Else():
                with act.Fori(0, NG) as g:
                    act.wait_ge(gen_lin, g + 1)
                    nc.scalar.activation(r_sb[:, 0, 0:GROUP], pa[0:M1, 0, :], ACT.Relu).then_inc(gen_relu, 1)
                    act.wait_ge(gen_pre, g + 1)
                    nc.scalar.activation(msg[:, 0, :, 0:C], pc[:, 0, 0:TPG * C].rearrange("p (t c) -> p t c", c=C),
                                         ACT.Relu).then_inc(gen_msg, 1)
                    act.wait_ge(gen_msg, g + 1)
                    nc.scalar.square(msg[:, 0, :, M1:MW], msg[:, 0, :, 0:C]).then_inc(gen_square, 1)

            act.wait_ge(sqrt_asked, 2)
            nc.scalar.sqrt(sc[:, 12:13], sc[:, 11:12]).then_inc(sqrt_done, 1)

        @block.tensor
        def _(pe):
            pe.wait_ge(consts_in, 16)

            def turn(q):
                chunk = max(c for c in range(N_LN + N_RAW) if q in ln_quads(c))
                pe.wait_ge(z_ready, chunk + 1)
                if ln_by_act(chunk):
                    pe.wait_ge(z_by_act, chunk + 1)
                wait(pe, h_kept, q - 1)
                for b in range(quad(q)):
                    last = nc.tensor.transpose(pb[0:C, q % 2, 128 * b:128 * b + 128], rows_of(q)[:, b, :], ident[:, :])
                last.then_inc(z_turned, 1)

            def table(q, w, made):
                for b in range(quad(q)):
                    last = nc.tensor.matmul(pc[:, q % 2, C * b:C * b + C], h_of(q)[:, 128 * b:128 * b + 128], w[:, :],
                                            start=True, stop=True)
                last.then_inc(made, 1)

            for q in range(NQ + RAW):
                if q in (0, NQ):
                    turn(q)
                if q + 1 not in (NQ, NQ + RAW):
                    turn(q + 1)
                pe.wait_ge(h_kept, q + 1)
                wait(pe, p_kept, q - 1)
                table(q, w1, p_made)
                if q == NQ - 1:
                    pe.wait_ge(bad_ready, 1)
                    nc.tensor.matmul(pd[0:1, 0, 0:2], ones[:, :], bad[:, 2:4], start=True,
                                     stop=True).then_inc(bad_counted, 1)
            pe.wait_ge(p_kept, NQ + RAW)
            pe.wait_ge(we_placed, 16 * len(STACK))

            def p1_unit(i, k):
                u = i * 4 + k
                pe.wait_ge(p1_x[k], i * 16 + 16)
                wait(pe, p1_relu, u - 1)
                for half in range(2):
                    last = nc.tensor.matmul((pa, pb)[k % 2][0:M1, half, :], we_stack[:, :],
                                            xs[:, k, half * GROUP:(half + 1) * GROUP], start=True, stop=True)
                last.then_inc(p1_lin, 1)
                for q in p1_quads(i, k):
                    wait(pe, q_kept, q - 1)
                    table(q, w2, q_made)

            def p1_body(i, units=4):
                for k in range(units):
                    p1_unit(i, k)
                wait(pe, node_relu, i)
                nc.tensor.matmul(pd[0:C, 0, 0:MLP_CHUNK], wn, h_t[:, bass.ds(i * MLP_CHUNK, MLP_CHUNK)],
                                 start=True, stop=True).then_inc(node_made, 1)

            p1_passes(pe, p1_body, lambda i: p1_body(i, P1_TAIL))
            pe.wait_ge(shift_ready, 1)
            nc.tensor.matmul(pd[0:M1, 0, 0:C], t_col[:, :], w3[:, :], start=True, stop=True).then_inc(shift_made, 1)

            pe.wait_ge(flag_ready, 1)
            outside = pe.value_load(flag[0:1, 0:1], min_val=0, max_val=2 * P)
            pe.wait_ge(main_ready, 1)
            with pe.If(outside < 1):
                def edges(i, j):
                    i, j = at(i, j)
                    if not exists(i, j):
                        return
                    g, n = num(i, j), tiles(i, j)
                    if j % 2 == 0:
                        pe.wait_ge(x_main[j // 2], i * 16 + 16)
                    wait(pe, edge_relu, g - 1)
                    nc.tensor.matmul(pa[0:M1, j % 2, 0:n * TILE], we_stack[:, :],
                                     xs[:, j // 2, j % 2 * GROUP:j % 2 * GROUP + n * TILE],
                                     start=True, stop=True).then_inc(edge_lin, 1)
                    pe.wait_ge(hot_built, g + 1)
                    wait(pe, hot_kept, g - 1)
                    for t in range(n):
                        last = nc.tensor.transpose(pb[0:WIN, j % 2, t * TILE:(t + 1) * TILE], hot[:, j, t, :],
                                                   ident[:, :])
                    last.then_inc(hot_turned, 1)

                def products(i, j):
                    i, j = at(i, j)
                    if not exists(i, j):
                        return
                    g, n = num(i, j), tiles(i, j)
                    pe.wait_ge(edge_relu, g + 1)
                    pe.wait_ge(hot_kept, g + 1)
                    pe.wait_ge(q_in[j], i * 16 + 16)
                    wait(pe, msg_relu, g - 1)
                    for t in range(n):
                        out = pc[:, j % 2, t * C:(t + 1) * C]
                        nc.tensor.matmul(out, r_sb[:, j % 2, t * TILE:(t + 1) * TILE], w3c[:, :],
                                         start=True, stop=False)
                        last = nc.tensor.matmul(out, hot_n[:, j % 2, t * TILE:(t + 1) * TILE], q_win[:, j, :],
                                                start=False, stop=True)
                    last.then_inc(pre_summed, 1)

                def window_sum(i, j):
                    g, n = num(i, j), tiles(i, j)
                    pe.wait_ge(msg_relu, g + 1)
                    wait(pe, win_added, g - 1)
                    for t in range(n):
                        last = nc.tensor.matmul(pd[0:M1, j % 2, 0:WIN], msg[:, j % 2, t, 0:M1], hot[:, j, t, :],
                                                start=(t == 0), stop=(t == n - 1))
                    last.then_inc(win_summed, 1)

                edges(0, 0)
                edges(0, 1)
                products(0, 0)

                def fast(i):
                    for j in range(BODY):
                        edges(i, j + 2)
                        products(i, j + 1)
                        window_sum(i, j)
                passes(pe, fast)
            with pe.Else():
                with pe.Fori(0, NG) as g:
                    pe.wait_ge(gen_turn, g + 1)
                    pe.wait_ge(gen_x, g * 16 + 16)
                    nc.tensor.matmul(pa[0:M1, 0, :], we_stack[:, :], xs[:, 0, 0:GROUP],
                                     start=True, stop=True).then_inc(gen_lin, 1)
                    pe.wait_ge(gen_relu, g + 1)
                    for t in range(TPG):
                        last = nc.tensor.matmul(pc[:, 0, t * C:(t + 1) * C], r_sb[:, 0, t * TILE:(t + 1) * TILE],
                                                w3c[:, :], start=True, stop=True)
                    last.then_inc(gen_sum, 1)
                    with pe.Fori(0, GEN_WINS) as w:
                        pe.wait_ge(gen_msg, g + 1)
                        pe.wait_ge(gen_hot, g * GEN_WINS + w + 1)
                        for t in range(TPG):
                            last = nc.tensor.matmul(pd[0:M1, 0, 0:WIN], msg[:, 0, t, 0:M1], hot[:, 0, t, :],
                                                    start=(t == 0), stop=(t == TPG - 1))
                        last.then_inc(gen_win, 1)

            pe.wait_ge(messages_done, 1)
            for k, lo in ((0, 0), (1, M1)):
                for t in range(TPG):
                    last = nc.tensor.matmul(pd[0:C, 0, k:k + 1], acc[:, t, lo:lo + C], ones[:, :],
                                            start=(t == 0), stop=(t == TPG - 1))
            last.then_inc(sums_made, 1)
            pe.wait_ge(fold_ready, 1)
            nc.tensor.transpose(pa[0:M1, 0, 0:C], fold[:, :], ident[0:C, 0:C]).then_inc(fold_turned, 1)
            pe.wait_ge(diag_kept, 1)
            for q in range(NQ):
                wait(pe, out_ready, q - 1)
                nc.tensor.matmul(pc[0:C, q % 2, 0:nodes(q)], s_diag[:, :], agg[:, 512 * q:512 * q + nodes(q)],
                                 start=True, stop=True).then_inc(out_made, 1)

        @block.vector
        def _(dve):
            steps = [0]

            def link(ins):
                steps[0] += 1
                ins.then_inc(dve_step, 1)
                dve.wait_ge(dve_step, steps[0])

            V = nc.vector
            dve.sem_inc(pre_added, RING)
            V.memset(ones[:, :], 1.0)
            V.memset(t_col[:, :], 0.0)
            V.memset(bad[:, :], 0.0)
            V.memset(acc[:, :, :], 0.0).then_inc(zeroed, 1)

            def ln_stats(c):
                rows, b0, n = ln_blocks(c)
                if c < N_LN:
                    dve.wait_ge(x_in[c], 16)
                else:
                    dve.wait_ge(raw_done[c - N_LN], 16 * RAW_CHUNK * TPG)
                for b in range(n):
                    last = V.bn_stats(ln_st[:, b0 + b, :], rows[:, b, :])
                link(last)
                st, w = ln_st[:, b0:b0 + n, :], ln_w[:, :, b0:b0 + n]
                V.tensor_tensor(w[:, 4, :], st[:, :, 1], st[:, :, 4], ALU.add)
                V.tensor_tensor(w[:, 1, :], st[:, :, 2], st[:, :, 5], ALU.add)
                link(V.tensor_tensor(w[:, 0, :], st[:, :, 1], st[:, :, 4], ALU.subtract))
                link(V.tensor_tensor(w[:, 0, :], w[:, 0, :], w[:, 0, :], ALU.mult))
                link(V.scalar_tensor_tensor(w[:, 1, :], w[:, 0, :], C / 4.0, w[:, 1, :], ALU.mult, ALU.add))
                V.tensor_scalar(w[:, 2, :], w[:, 1, :], 1.0 / C, EPS, ALU.mult, ALU.add).then_inc(ln_var, 1)
                V.tensor_scalar(w[:, 4, :], w[:, 4, :], 0.5, None, ALU.mult)

            def ln_apply(c):
                rows, b0, n = ln_blocks(c)
                cols = slice(b0, b0 + n)
                dve.wait_ge(ln_sqrt, c + 1)
                link(V.reciprocal(ln_rstd[:, cols], ln_rstd[:, cols]))
                if ln_by_act(c):
                    V.scalar_tensor_tensor(ln_shift[:, cols], ln_mean[:, cols], -1.0, ln_rstd[:, cols], ALU.mult,
                                           ALU.mult).then_inc(z_scales, 1)
                for b in range(ln_by_act(c), n):
                    last = V.tensor_scalar(rows[:, b, :], rows[:, b, :], ln_mean[:, b0 + b:b0 + b + 1],
                                           ln_rstd[:, b0 + b:b0 + b + 1], ALU.subtract, ALU.mult)
                last.then_inc(z_ready, 1)

            def take_off(s):
                dve.wait_ge(split_step, 2 * s + 1)
                V.tensor_tensor(edge_f, edge_f, splits[:, s, :], ALU.subtract).then_inc(split_step, 1)

            ln_stats(0)
            for c in range(N_LN):
                if c + 1 < N_LN:
                    ln_stats(c + 1)
                ln_apply(c)

            dve.wait_ge(we_in, 16)
            dve.wait_ge(consts_in, 16)
            link(V.tensor_copy(we_split[:, 0, :], we5[:, :]))
            link(V.tensor_tensor(we5[:, :], we5[:, :], we_split[:, 0, :], ALU.subtract))
            link(V.tensor_copy(we_split[:, 1, :], we5[:, :]))
            link(V.tensor_tensor(we5[:, :], we5[:, :], we_split[:, 1, :], ALU.subtract))
            V.tensor_copy(we_split[:, 2, :], we5[:, :]).then_inc(we_ready, 1)

            dve.wait_ge(dst_in, 32)
            rel = dst_rel[:, :, :].rearrange("p g t -> p (g t)")
            far = msg[:, :, :, :].rearrange("p a t w -> p (a t w)")[:, 0:NTILES]
            link(V.tensor_tensor(dst_rel[:, :, :], dst_i[:, 0:NTILES].rearrange("p (g t) -> p g t", t=TPG),
                                 base_b[:, :].unsqueeze(2).to_broadcast([P, NG, TPG]), ALU.subtract))
            full = (NG - 1) * TPG + LAST_TILES - 1
            link(V.tensor_scalar(far, rel, -(WIN - 1) / 2.0, None, ALU.add))
            link(V.tensor_tensor(far, far, far, ALU.mult))
            V.tensor_reduce(bad[:, 0:1], far[:, 0:full], AX, ALU.max)
            link(V.tensor_copy(bad[0:LAST_ROWS, 1:2], far[0:LAST_ROWS, full:full + 1]))
            V.tensor_scalar(bad[:, 2:4], bad[:, 0:2], (WIN / 2.0) ** 2, None, ALU.is_gt).then_inc(bad_ready, 1)
            for k in range(2):
                V.memset(msg[:, k, :, C:M1], 1.0)

            ln_stats(N_LN)
            dve.wait_ge(bad_counted, 1)
            V.tensor_reduce(flag[0:1, 0:1], pd[0:1, 0, 0:2], AX, ALU.max).then_inc(flag_ready, 1)
            for c in range(N_LN, N_LN + N_RAW):
                if c + 1 < N_LN + N_RAW:
                    ln_stats(c + 1)
                ln_apply(c)
                if c == N_LN:
                    take_off(0)
                if c == N_LN + 1:
                    take_off(1)
            def p1_body(i, units=4):
                for k in range(units):
                    u = i * 4 + k
                    dve.wait_ge(p1_relu, u + 1)
                    for half in range(2):
                        n = LAST_EDGES if isinstance(i, int) and 2 * u + half == NG - 1 else GROUP
                        last = V.bn_stats(edge_st[:, bass.ds(u * 2 + half, 1), :].rearrange("c a s -> c (a s)"),
                                          r_sb[0:C, k % 2, half * GROUP:half * GROUP + n])
                    last.then_inc(p1_stat, 1)
                dve.wait_ge(node_relu, i + 1)
                V.bn_stats(node_st[:, bass.ds(i, 1), :].rearrange("c a s -> c (a s)"),
                           node_t[:, bass.ds(i * MLP_CHUNK, MLP_CHUNK)]).then_inc(node_stat, 1)

            p1_passes(dve, p1_body, lambda i: p1_body(i, P1_TAIL))
            dve.wait_ge(node_stat, P1_LOOPS + 1)
            V.bn_aggr(sc[:, 6:8], node_st[:, :, :].rearrange("c q s -> c (q s)"))
            dve.wait_ge(p1_stat, NG // 2)
            link(V.bn_aggr(sc[:, 0:2], edge_st[:, :, :].rearrange("c g s -> c (g s)")))
            V.tensor_scalar(sc[:, 2:3], sc[:, 1:2], EPS, None, ALU.add)
            V.tensor_scalar(sc[:, 3:4], sc[:, 7:8], EPS, None, ALU.add).then_inc(sqrt_asked, 1)
            dve.wait_ge(sqrt_done, 1)
            link(V.reciprocal(sc[:, 4:6], sc[:, 4:6]))
            V.tensor_tensor(sc[:, 8:9], sc[:, 4:5], vec[:, G_EDGE:G_EDGE + 1], ALU.mult)
            link(V.tensor_tensor(sc[:, 10:11], sc[:, 5:6], vec[:, G_NODE:G_NODE + 1], ALU.mult))
            V.tensor_scalar(w3c[0:C, :], w3[:, :], sc[:, 8:9], None, ALU.mult)
            V.tensor_tensor(sc[:, 9:10], sc[:, 0:1], sc[:, 8:9], ALU.mult)
            link(V.tensor_tensor(sc[:, 13:14], sc[:, 6:7], sc[:, 10:11], ALU.mult))
            V.tensor_tensor(t_col[:, C:M1], vec[:, BT_EDGE:BT_EDGE + 1], sc[:, 9:10],
                            ALU.subtract).then_inc(shift_ready, 1)
            link(V.tensor_tensor(sc[:, 14:15], vec[:, BT_NODE:BT_NODE + 1], sc[:, 13:14], ALU.subtract))
            V.memset(fold[:, :], 0.0)
            dve.wait_ge(agg_zeroed, 16)
            dve.wait_ge(p_kept, NQ + RAW)
            dve.wait_ge(shift_made, 1)
            V.tensor_tensor(w3c[C:M1, :], pd[C:M1, 0, 0:C], bm_row[C:M1, :], ALU.add).then_inc(main_ready, 1)

            def add_node(i):
                n = node_cols(i)
                part = node_t[:, bass.ds(i * NODE_CHUNK, n)]
                dve.wait_ge(res_in, i * 16 + 16)
                V.scalar_tensor_tensor(part, part, sc[:, 10:11], res[:, 0:n], ALU.mult,
                                       ALU.add).then_inc(node_added, 1)

            outside = dve.value_load(flag[0:1, 0:1], min_val=0, max_val=2 * P)
            with dve.If(outside < 1):
                def build_hot(i, j):
                    i, j = at(i, j)
                    if not exists(i, j):
                        return
                    g, n = num(i, j), tiles(i, j)
                    wait(dve, win_summed, g - 3)
                    V.tensor_tensor(hot[:, j, 0:n, :],
                                    dst_rel[:, bass.ds(g, 1), 0:n].rearrange("p a t -> p (a t)").unsqueeze(2).to_broadcast([P, n, WIN]),
                                    ramp[:, :].unsqueeze(1).to_broadcast([P, n, WIN]),
                                    ALU.is_equal).then_inc(hot_built, 1)

                def add_gathered(i, j):
                    i, j = at(i, j)
                    if not exists(i, j):
                        return
                    g, n = num(i, j), tiles(i, j) * C
                    dve.wait_ge(pre_summed, g + 1)
                    dve.wait_ge(gathered, g + 1)
                    V.tensor_tensor(pc[:, j % 2, 0:n], pc[:, j % 2, 0:n],
                                    ring[:, bass.ds((g % RING) * (TPG * C), n)], ALU.add).then_inc(pre_added, 1)

                def add_sums(i, j):
                    g, n = num(i, j), tiles(i, j)
                    base = dve.value_load(base_b[0:1, bass.ds(g, 1)], min_val=0, max_val=N - 1)
                    dve.wait_ge(msg_square, g + 1)
                    wait(dve, acc_added, g)
                    V.tensor_tensor(acc[:, 0:n, :], acc[:, 0:n, :], msg[:, j % 2, 0:n, :],
                                    ALU.add).then_inc(acc_added, 1)
                    dve.wait_ge(win_summed, g + 1)
                    wait(dve, win_added, g)
                    V.tensor_tensor(agg[:, bass.ds(base, WIN)], agg[:, bass.ds(base, WIN)], pd[0:M1, j % 2, 0:WIN],
                                    ALU.add).then_inc(win_added, 1)

                for j in range(3):
                    build_hot(0, j)
                add_gathered(0, 0)

                def fast(i):
                    for j in range(BODY):
                        build_hot(i, j + 3)
                        add_gathered(i, j + 1)
                        add_sums(i, j)
                    add_node(i)
                passes(dve, fast)
                dve.wait_ge(acc_added, NG)
                dve.wait_ge(win_added, NG)
            with dve.Else():
                dve.sem_inc(gen_turn, 1)
                far4 = bad[:, 0:TPG]
                with dve.Fori(0, NG) as g:
                    dve.wait_ge(gen_dst, g * 16 + 16)
                    V.tensor_copy(far4, dst_i2[:, 0:TPG]).then_inc(gen_step, 1)
                    dve.wait_ge(gen_sum, g + 1)
                    dve.wait_ge(gen_rows, g * (32 * TPG) + 32 * TPG)
                    per = GEN_WINS * 2 + 3
                    V.tensor_tensor(pc[:, 0, 0:TPG * C], pc[:, 0, 0:TPG * C], ring[:, 0:TPG * C],
                                    ALU.add).then_inc(gen_step, 1)
                    dve.wait_ge(gen_step, g * per + 2)
                    V.tensor_tensor(pc[:, 0, 0:TPG * C], pc[:, 0, 0:TPG * C], ring[:, TPG * C:2 * TPG * C],
                                    ALU.add).then_inc(gen_pre, 1)
                    dve.wait_ge(gen_square, g + 1)
                    V.tensor_tensor(acc[:, :, :], acc[:, :, :], msg[:, 0, :, :], ALU.add).then_inc(gen_step, 1)
                    with dve.Fori(0, GEN_WINS) as w:
                        V.tensor_tensor(hot[:, 0, :, :], far4.unsqueeze(2).to_broadcast([P, TPG, WIN]),
                                        ramp[:, :].unsqueeze(1).to_broadcast([P, TPG, WIN]),
                                        ALU.is_equal).then_inc(gen_hot, 1)
                        dve.wait_ge(gen_win, g * GEN_WINS + w + 1)
                        V.tensor_scalar(far4, far4, -float(WIN), None, ALU.add).then_inc(gen_step, 1)
                        V.tensor_tensor(agg[:, bass.ds(w * WIN, WIN)], agg[:, bass.ds(w * WIN, WIN)],
                                        pd[0:M1, 0, 0:WIN], ALU.add).then_inc(gen_step, 1)
                        dve.wait_ge(gen_step, g * per + w * 2 + 5)
                    V.memset(flag[0:1, 0:1], 0).then_inc(gen_turn, 1)
                dve.wait_ge(gen_turn, NG + 1)
                passes(dve, add_node)

            dve.sem_inc(messages_done, 1)
            dve.wait_ge(sums_made, 1)
            link(V.tensor_scalar(sc[:, 0:2], pd[0:C, 0, 0:2], 1.0 / E, None, ALU.mult))
            link(V.tensor_tensor(sc[:, 2:3], sc[:, 0:1], sc[:, 0:1], ALU.mult))
            link(V.tensor_tensor(sc[:, 3:4], sc[:, 1:2], sc[:, 2:3], ALU.subtract))
            V.tensor_scalar(sc[:, 11:12], sc[:, 3:4], 0.0, EPS, ALU.max, ALU.add).then_inc(sqrt_asked, 1)
            dve.wait_ge(sqrt_done, 2)
            link(V.reciprocal(sc[:, 12:13], sc[:, 12:13]))
            link(V.tensor_tensor(sc[:, 8:9], sc[:, 12:13], vec[:, G_MSG:G_MSG + 1], ALU.mult))
            V.tensor_scalar(fold[:, 0:C], ident[0:C, 0:C], sc[:, 8:9], None, ALU.mult)
            link(V.tensor_tensor(sc[:, 9:10], sc[:, 0:1], sc[:, 8:9], ALU.mult))
            V.tensor_tensor(fold[:, C:M1], vec[:, BT_MSG:BT_MSG + 1], sc[:, 9:10],
                            ALU.subtract).then_inc(fold_ready, 1)
            dve.wait_ge(fold_turned, 1)
            V.tensor_copy(s_diag[:, :], pa[0:M1, 0, 0:C]).then_inc(diag_kept, 1)
            dve.wait_ge(node_added, LOOPS)
            for q in range(NQ):
                dve.wait_ge(out_made, q + 1)
                part = node_t[:, 512 * q:512 * q + nodes(q)]
                V.scalar_tensor_tensor(part, pc[0:C, q % 2, 0:nodes(q)], sc[:, 14:15], part, ALU.add,
                                       ALU.add).then_inc(out_ready, 1)


def kernel(**inputs):
    import numpy as _np
    import concourse.bacc as _bacc
    from concourse import mybir as _mybir
    from concourse.bass_utils import run_bass_kernel_spmd as _run

    x, src, dst, ea = (_np.asarray(inputs[k]) for k in ("x", "src", "dst", "edge_attr_4"))
    w = {k[7:]: _np.asarray(v) for k, v in inputs.items() if k.startswith("L0_gnn_")}
    x_pad = _np.zeros((NP, C), x.dtype)
    x_pad[:N] = x
    src_pad = _np.full(IDX_W * TILE, N, src.dtype)
    src_pad[:E] = src
    dst_pad = _np.full(EP, N, dst.dtype)
    dst_pad[:E] = dst
    rows = _np.zeros((EROWS, EP), ea.dtype)
    rows[0, :E] = 1.0
    rows[1:, :E] = ea.T
    packed = _np.zeros((P, PACKED), _np.float32)
    packed[:, 0:P] = _np.eye(P)
    packed[:, RAMP_AT:RAMP_AT + WIN] = _np.arange(WIN)
    for k, part in enumerate((w["W_node"], w["W_msg"][:C], w["W_msg"][C:2 * C], w["W_msg"][2 * C:])):
        packed[:C, WN_AT + k * C:WN_AT + (k + 1) * C] = part
    packed[C, BM_AT:BM_AT + C] = w["b_msg"]
    for k, name in enumerate(("b_node", "g_node", "beta_node", "g_edge", "beta_edge", "g_msg", "beta_msg")):
        packed[:C, VEC_AT + k] = w[name]
    w_edge = _np.zeros((EROWS, M1), _np.float32)
    w_edge[0, :C] = w["b_edge"]
    w_edge[0, C] = 1.0
    w_edge[1:, :C] = w["W_edge"]
    arrays = {
        "x_rows": x,
        "x_nodes": x_pad.reshape(NB, P, C).transpose(1, 0, 2),
        "x_t": x.T,
        "src_cols": src_pad.reshape(IDX_W, TILE).T,
        "dst_cols": dst_pad.reshape(NTILES, TILE).T,
        "group_base": dst_pad[::GROUP],
        "edge_rows": rows.reshape(P, SPLIT_F),
        "packed": packed,
        "w_edge": w_edge,
    }
    nc = _bacc.Bacc("TRN2", target_bir_lowering=False, num_devices=1)
    args = []
    for name in list(arrays):
        a = arrays["in_" + name] = _np.ascontiguousarray(arrays.pop(name))
        args.append(nc.dram_tensor("in_" + name, a.shape, _mybir.dt.from_np(a.dtype), kind="ExternalInput").ap())
    args.append(nc.dram_tensor("out_t", (C, N), _mybir.dt.float32, kind="ExternalOutput").ap())
    graph_layer(nc, *args)
    r = _run(nc, [arrays], core_ids=[0])
    return _np.ascontiguousarray(r.results[0]["out_t"].T)
```

```python
import concourse.bass as bass
from concourse import mybir
from contextlib import ExitStack

N, E, C, EF = 6250, 100000, 96, 4
P = 128
TILE = P
TPG = 4
GROUP = TPG * TILE
NG = -(-E // GROUP)
NTILES = NG * TPG
LAST_EDGES = E - (NG - 1) * GROUP
LAST_TILES = -(-LAST_EDGES // TILE)
LAST_ROWS = LAST_EDGES - (LAST_TILES - 1) * TILE
EP = NG * GROUP
WIN = 96
NB = -(-(N + WIN) // P)
NP = NB * P
NQ = -(-NB // 4)
EPS = 1e-5
STACK = (("hi", "hi"), ("hi", "mid"), ("hi", "lo"), ("mid", "hi"), ("mid", "mid"), ("lo", "hi"))
EROWS = EF + 1
KROWS = len(STACK) * EROWS
SPLIT_F = EROWS * EP // P
BODY = 4
LOOPS = NG // BODY
RAW = 12
RING = 60
ROUNDS = (NG - RAW) // RING
AHEAD = 3
IDX_W = (RING + NG) * TPG
LN_CHUNK = 10
RAW_CHUNK = 2
NODE_CHUNK = -(-N // LOOPS)
GEN_WINS = -(-N // WIN)
M1 = C + 1
RAMP_AT = P
WN_AT = RAMP_AT + WIN
BM_AT = WN_AT + 4 * C
VEC_AT = BM_AT + C
PACKED = VEC_AT + 7
P1_LOOPS = NG // 8
P1_TAIL = NG % 8 // 2
Q_LOOPS = 3
RAW_LOOPS = 3
P1_PEELED = Q_LOOPS + RAW_LOOPS
MLP_CHUNK = N // (P1_LOOPS + 1)
MW = C + 1 + C
W_GATHER, W_SUMS, W_SCALES, W_DIAG = (8, 4), 5, 9, 2


def graph_layer(nc, x_rows, x_nodes, x_t, src_cols, dst_cols, group_base, edge_rows, packed, w_edge, out_t):
    fp32, bf16, i32 = mybir.dt.float32, mybir.dt.bfloat16, mybir.dt.int32
    ALU, ACT, AX = mybir.AluOpType, mybir.ActivationFunctionType, mybir.AxisListType.X

    p_table = nc.dram_tensor("p_table", (NP, C), fp32, kind="Internal").ap()
    q_table = nc.dram_tensor("q_table", (NP, C), fp32, kind="Internal").ap()
    x_stack = nc.dram_tensor("x_stack", (KROWS, EP), bf16, kind="Internal").ap()

    with ExitStack() as ctx:
        def sb(name, shape, dt=fp32):
            return ctx.enter_context(nc.sbuf_tensor(name, shape, dt))

        def sem(name):
            return ctx.enter_context(nc.semaphore(name))

        ring = sb("ring", [P, RING * TPG * C])
        splits_at = RING * TPG * C - -(-3 * SPLIT_F // 2)
        node_at = splits_at - NB * C
        splits_slot, node_slot = splits_at // (TPG * C), node_at // (TPG * C)
        zn = ring[:, node_at:splits_at].rearrange("p (b c) -> p b c", c=C)
        raw = ring[:, 0:RAW * TPG * C].rearrange("p (b c) -> p b c", c=C)
        splits = ring[:, splits_at:splits_at + 3 * SPLIT_F // 2].bitcast(bf16).rearrange("p (s f) -> p s f", s=3)
        big_a = sb("big_a", [P, NP])
        h_t, agg = big_a[:, :], big_a[0:M1, :]
        big_b = sb("big_b", [P, N])
        node_t, edge_f = big_b[0:C, :], big_b[:, 0:SPLIT_F]
        res = sb("res", [C, NODE_CHUNK])
        xs = sb("xs", [P, 4, 2 * GROUP], bf16)
        src_slots = sb("src_slots", [P, RING * TPG], i32)
        src_later = sb("src_later", [P, NG * TPG], i32)
        dst_rel = sb("dst_rel", [P, NG, TPG])
        base_b = sb("base_b", [P, NG], i32)
        hot = sb("hot", [P, 4, TPG, WIN])
        dst_i = hot[:, :, :, :].bitcast(i32).rearrange("p a t w -> p (a t w)")
        dst_i2 = hot[:, 2:4, :, :].bitcast(i32).rearrange("p a t w -> p (a t w)")
        r_sb = sb("r_sb", [P, 2, 2 * GROUP])
        hot_n = sb("hot_n", [P, 2, GROUP])
        msg = sb("msg", [P, 2, TPG, MW])
        acc = sb("acc", [P, TPG, MW])
        edge_st = sb("edge_st", [C, NG, 6])
        node_st = sb("node_st", [C, P1_LOOPS + 1, 6])
        ln_buf = sb("ln_buf", [P, 2, 6 * (NB + RAW * TPG)])
        ln_st = ln_buf[:, 0, :].rearrange("p (b s) -> p b s", s=6)
        ln_w = ln_buf[:, 1, :].rearrange("p (s b) -> p s b", s=6)
        hot_b = ln_buf[:, :, :].rearrange("p a f -> p (a f)")[:, 0:2 * TPG * WIN].bitcast(bf16).rearrange(
            "p (a t w) -> p a t w", a=4, w=WIN)
        ident_b = sb("ident_b", [P, P], bf16)
        q_win = sb("q_win", [P, 4, C])
        ones = sb("ones", [P, 1])
        pk = sb("pk", [P, PACKED])
        ident, ramp = pk[:, 0:P], pk[:, RAMP_AT:RAMP_AT + WIN]
        wn, w1, w2 = (pk[:, WN_AT + k * C:WN_AT + (k + 1) * C] for k in range(3))
        w3 = pk[0:C, WN_AT + 3 * C:WN_AT + 4 * C]
        bm_row, vec = pk[0:M1, BM_AT:BM_AT + C], pk[0:C, VEC_AT:VEC_AT + 7]
        w3c = sb("w3c", [P, C])
        we5 = sb("we5", [EROWS, M1])
        we_split = sb("we_split", [EROWS, 3, M1], bf16)
        we_stack = sb("we_stack", [P, M1], bf16)
        sc = sb("sc", [C, 16])
        t_col = sb("t_col", [C, M1])
        fold = sb("fold", [C, M1])
        s_diag = sb("s_diag", [M1, C])
        bad = sb("bad", [P, 4])
        flag = sb("flag", [1, 1], i32)
        ln_rstd, ln_mean, ln_shift = ln_w[:, 3, :], ln_w[:, 4, :], ln_w[:, 5, :]

        pa = ctx.enter_context(nc.psum_tensor("pa", [P, 2, 512], fp32))
        pb = ctx.enter_context(nc.psum_tensor("pb", [P, 2, 512], fp32))
        pc = ctx.enter_context(nc.psum_tensor("pc", [P, 2, 512], fp32))
        pd = ctx.enter_context(nc.psum_tensor("pd", [P, 2, 512], fp32))
        pb_b = pb[:, :, :].bitcast(bf16)

        B_NODE, G_NODE, BT_NODE, G_EDGE, BT_EDGE, G_MSG, BT_MSG = range(7)

        x_in = [sem(f"x_in{c}") for c in range(NB // LN_CHUNK)]
        edge_in = sem("edge_in")
        consts_in = sem("consts_in")
        we_in = sem("we_in")
        dst_in = sem("dst_in")
        src_first = sem("src_first")
        src_in = sem("src_in")
        zeroed = sem("zeroed")
        h_zeroed = sem("h_zeroed")
        rows_cleared = sem("rows_cleared")
        dve_step = sem("dve_step")
        ln_var = sem("ln_var")
        ln_sqrt = sem("ln_sqrt")
        z_ready = sem("z_ready")
        z_turned = sem("z_turned")
        z_scales = sem("z_scales")
        z_by_act = sem("z_by_act")
        h_kept = sem("h_kept")
        p_made = sem("p_made")
        p_kept = sem("p_kept")
        p_stored = sem("p_stored")
        q_made = sem("q_made")
        q_kept = sem("q_kept")
        q_stored = sem("q_stored")
        node_made = sem("node_made")
        node_relu = sem("node_relu")
        node_stat = sem("node_stat")
        split_step = sem("split_step")
        raw_done = [sem(f"raw_done{k}") for k in range(RAW // RAW_CHUNK)]
        agg_zeroed = sem("agg_zeroed")
        stack_stored = sem("stack_stored")
        we_ready = sem("we_ready")
        we_placed = sem("we_placed")
        bad_ready = sem("bad_ready")
        bad_counted = sem("bad_counted")
        flag_ready = sem("flag_ready")
        res_in = sem("res_in")
        sqrt_asked = sem("sqrt_asked")
        sqrt_done = sem("sqrt_done")
        shift_ready = sem("shift_ready")
        shift_made = sem("shift_made")
        p1_x = [sem(f"p1_x{k}") for k in range(4)]
        p1_lin = sem("p1_lin")
        p1_relu = sem("p1_relu")
        p1_stat = sem("p1_stat")
        main_ready = sem("main_ready")
        slot_free = sem("slot_free")
        gather_done = [sem(f"gather_done{k}") for k in range(4)]
        gathered = sem("gathered")
        x_main = [sem(f"x_main{k}") for k in range(2)]
        q_in = [sem(f"q_in{k}") for k in range(4)]
        edge_lin = sem("edge_lin")
        edge_relu = sem("edge_relu")
        turn_built = sem("turn_built")
        hot_built = sem("hot_built")
        hot_turned = sem("hot_turned")
        hot_kept = sem("hot_kept")
        pre_summed = sem("pre_summed")
        pre_added = sem("pre_added")
        msg_relu = sem("msg_relu")
        msg_square = sem("msg_square")
        win_summed = sem("win_summed")
        win_added = sem("win_added")
        acc_added = sem("acc_added")
        node_added = sem("node_added")
        gen_turn = sem("gen_turn")
        gen_x = sem("gen_x")
        gen_rows = sem("gen_rows")
        gen_claimed = sem("gen_claimed")
        gen_lin = sem("gen_lin")
        gen_relu = sem("gen_relu")
        gen_sum = sem("gen_sum")
        gen_dst = sem("gen_dst")
        gen_pre = sem("gen_pre")
        gen_msg = sem("gen_msg")
        gen_square = sem("gen_square")
        gen_hot = sem("gen_hot")
        gen_win = sem("gen_win")
        gen_step = sem("gen_step")
        messages_done = sem("messages_done")
        sums_made = sem("sums_made")
        fold_ready = sem("fold_ready")
        fold_turned = sem("fold_turned")
        diag_kept = sem("diag_kept")
        out_made = sem("out_made")
        out_ready = sem("out_ready")
        out_stored = sem("out_stored")

        N_LN = NB // LN_CHUNK
        N_RAW = RAW // RAW_CHUNK
        N_RAW_EARLY = N_RAW - Q_LOOPS

        def at(i, j):
            return i + j // BODY, j % BODY

        def num(i, j):
            return i * BODY + j

        def exists(i, j):
            return not isinstance(i, int) or 0 <= num(i, j) < NG

        def wait(eng, s, value):
            if not isinstance(value, int) or value > 0:
                eng.wait_ge(s, value)

        def tiles(i, j):
            return LAST_TILES if isinstance(i, int) and num(i, j) == NG - 1 else TPG

        def passes(eng, body):
            body(0)
            with eng.Fori(1, LOOPS - 1) as i:
                body(i)
            body(LOOPS - 1)

        assert MLP_CHUNK * (P1_LOOPS + 1) == N and NQ <= 4 * Q_LOOPS + 1
        assert RAW == 4 * RAW_LOOPS and N_RAW == N_RAW_EARLY + Q_LOOPS

        def p1_passes(eng, body, tail):
            for i in range(P1_PEELED):
                body(i)
            with eng.Fori(P1_PEELED, P1_LOOPS) as i:
                body(i)
            tail(P1_LOOPS)

        def p1_quads(i, k):
            if not isinstance(i, int) or i >= Q_LOOPS:
                return []
            u = 4 * i + k
            return [q for q in (u, u + 1) if q < NQ and (q == u or u == 4 * Q_LOOPS - 1)]

        def p1_raw_turn(i, k):
            return [NQ + 4 * (i - Q_LOOPS) + k] if isinstance(i, int) and Q_LOOPS <= i < P1_PEELED else []

        def p1_raw_table(i, k):
            return [q for t in p1_raw_turn(i, k) for q in (t - 1, t) if q >= NQ and (q < t or t == NQ + RAW - 1)]

        def p1_raw_ln(i):
            return [N_LN + N_RAW_EARLY + i] if isinstance(i, int) and i < Q_LOOPS else []

        def node_cols(i):
            return min(NODE_CHUNK, N - i * NODE_CHUNK) if isinstance(i, int) else NODE_CHUNK

        def quad(q):
            return min(4, NB - 4 * q) if q < NQ else TPG

        def rows_of(q):
            return zn[:, 4 * q:4 * q + quad(q), :] if q < NQ else raw[:, (q - NQ) * TPG:(q - NQ + 1) * TPG, :]

        def h_of(q):
            return h_t[:, 512 * q:512 * q + 128 * quad(q)] if q < NQ else hot_n[:, q % 2, :]


        def turned(q):
            return pb[0:C, q % 2, 0:128 * quad(q)] if q < NQ else pd[0:C, 1, :]

        def ln_blocks(c):
            if c < N_LN:
                return zn[:, c * LN_CHUNK:(c + 1) * LN_CHUNK, :], c * LN_CHUNK, LN_CHUNK
            k = (c - N_LN) * RAW_CHUNK * TPG
            return raw[:, k:k + RAW_CHUNK * TPG, :], NB + k, RAW_CHUNK * TPG

        def ln_quads(c):
            if c >= N_LN:
                return range(NQ + (c - N_LN) * RAW_CHUNK, NQ + (c - N_LN + 1) * RAW_CHUNK)
            return [q for q in range(NQ) if c * LN_CHUNK < 4 * q + quad(q) <= (c + 1) * LN_CHUNK]

        def ln_by_act(c):
            return LN_CHUNK // 2 if c < N_LN else 0

        def nodes(q):
            return min(512, N - 512 * q)

        def out_bank(q):
            return (pc, pb)[q % 4 // 2][0:C, q % 2, 0:nodes(q)]

        block = ctx.enter_context(nc.Block())

        @block.sync
        def _(sp):
            def stack_rows(k):
                rows = x_stack[k * EROWS:(k + 1) * EROWS, :].rearrange("r e -> (r e)")
                return rows.rearrange("(p f) -> p f", p=P)

            sp.dma_start(src_slots[:, 0:RAW * TPG], src_cols[:, 0:RAW * TPG]).then_inc(src_first, 16)
            for c in range(NB // LN_CHUNK):
                b0 = c * LN_CHUNK
                sp.dma_start(zn[:, b0:b0 + LN_CHUNK, :], x_nodes[:, b0:b0 + LN_CHUNK, :]).then_inc(x_in[c], 16)
            sp.wait_ge(zeroed, 1)
            sp.dma_start(big_a[C:P, :].rearrange("c (a b) -> c a b", b=NP // 10),
                         acc[0:P - C, :, :].rearrange("c t m -> c (t m)")[:, 0:NP // 10].unsqueeze(1).to_broadcast(
                             [P - C, 10, NP // 10])).then_inc(h_zeroed, 16)
            sp.dma_start(edge_f, edge_rows).then_inc(edge_in, 16)
            for q in range(NQ):
                sp.wait_ge(p_kept, q + 1)
                sp.dma_start(p_table[512 * q:512 * q + 128 * quad(q), :].rearrange("(b p) c -> p b c", p=P),
                             zn[:, 4 * q:4 * q + quad(q), :]).then_inc(p_stored, 16)
            for s, name in enumerate(("hi", "mid", "lo")):
                sp.wait_ge(split_step, 2 * s + 1)
                for k, (part, _) in enumerate(STACK):
                    if part == name:
                        sp.dma_start(stack_rows(k), splits[:, s, :]).then_inc(stack_stored, 16)
            sp.wait_ge(stack_stored, 16 * len(STACK))
            sp.wait_ge(rows_cleared, 1)

            def load_p1(i, units=4):
                for k in range(units):
                    u = i * 4 + k
                    wait(sp, p1_lin, u - 3)
                    sp.dma_start(xs[0:KROWS, k, :], x_stack[:, bass.ts(u, 2 * GROUP)]).then_inc(p1_x[k], 16)
                if isinstance(i, int) and 0 < i <= Q_LOOPS:
                    for q in [q for j in range(4) for q in p1_quads(i - 1, j)]:
                        sp.wait_ge(q_kept, q + 1)
                        sp.dma_start(q_table[512 * q:512 * q + 128 * quad(q), :].rearrange("(b p) c -> p b c", p=P),
                                     rows_of(q)).then_inc(q_stored, 16)

            for i in range(P1_PEELED + 1):
                load_p1(i)
            with sp.Fori(P1_PEELED + 1, P1_LOOPS) as i:
                load_p1(i)
            load_p1(P1_LOOPS, P1_TAIL)
            sp.wait_ge(node_made, P1_LOOPS + 1)
            sp.wait_ge(zeroed, 1)
            sp.dma_start(agg.rearrange("c (a b) -> c a b", b=NP // 10),
                         acc[0:M1, :, :].rearrange("c t m -> c (t m)")[:, 0:NP // 10].unsqueeze(1).to_broadcast(
                             [M1, 10, NP // 10])).then_inc(agg_zeroed, 16)

            def load_res(i):
                wait(sp, node_added, i)
                n = node_cols(i)
                sp.dma_start(res[:, 0:n], x_t[:, bass.ds(i * NODE_CHUNK, n)]).then_inc(res_in, 16)

            sp.wait_ge(p1_lin, NG // 2)
            sp.wait_ge(q_stored, 16 * NQ)
            sp.wait_ge(flag_ready, 1)
            outside = sp.value_load(flag[0:1, 0:1], min_val=0, max_val=2 * P)
            with sp.If(outside < 1):
                def fast(i):
                    for j in range(BODY):
                        g = num(i, j)
                        if j % 2 == 0:
                            wait(sp, edge_lin, g - 2)
                            sp.dma_start(xs[0:KROWS, j // 2, :], x_stack[:, bass.ds(g * GROUP, 2 * GROUP)]).then_inc(
                                x_main[j // 2], 16)
                        wait(sp, pre_summed, g - 3)
                        base = sp.value_load(base_b[0:1, bass.ds(g, 1)], min_val=0, max_val=N - 1)
                        sp.dma_start(q_win[0:WIN, j, :], q_table[bass.ds(base, WIN), :]).then_inc(q_in[j], 16)
                    load_res(i)
                passes(sp, fast)
            with sp.Else():
                with sp.Fori(0, NG) as g:
                    sp.wait_ge(gen_turn, g + 1)
                    sp.dma_start(xs[0:KROWS, 0, 0:GROUP], x_stack[:, bass.ds(g * GROUP, GROUP)]).then_inc(gen_x, 16)
                    sp.dma_start(dst_i2[:, 0:TPG], dst_cols[:, bass.ds(g * TPG, TPG)]).then_inc(gen_dst, 16)
                    sp.dma_start(src_slots[:, 0:TPG], src_cols[:, bass.ds(g * TPG, TPG)]).then_inc(gen_dst, 16)
                passes(sp, load_res)

            for q in range(NQ):
                sp.wait_ge(out_ready, q + 1)
                sp.dma_start(out_t[:, 512 * q:512 * q + nodes(q)], node_t[:, 512 * q:512 * q + nodes(q)]).then_inc(
                    out_stored, 16)
            sp.wait_ge(out_stored, 16 * NQ)

        @block.gpsimd
        def _(pool):
            def gather(slot, table, done, n=TPG):
                for t in range(n):
                    tile = slot * TPG + t
                    row_gather(tile, table, src_slots[:, tile:tile + 1], done)

            def row_gather(tile, table, idx, done):
                nc.gpsimd.indirect_dma_start(
                    out=ring[:, tile * C:(tile + 1) * C], out_offset=None, in_=table,
                    in_offset=bass.IndirectOffsetOnAxis(ap=idx, axis=0)).then_inc(done, 16)

            pool.wait_ge(src_first, 16)
            for g in range(RAW):
                gather(g, x_rows, raw_done[g // RAW_CHUNK])
            pool.sem_inc(gathered, RAW)
            pool.wait_ge(src_in, 32)
            pool.wait_ge(p_stored, 16 * NQ)
            pool.wait_ge(flag_ready, 1)
            outside = pool.value_load(flag[0:1, 0:1], min_val=0, max_val=2 * P)
            with pool.If(outside < 1):
                for g in range(RAW, RAW + AHEAD):
                    gather(g, p_table, gather_done[g % 4])
                with pool.Fori(0, ROUNDS) as r:
                    for k in range(RING):
                        start = RAW + AHEAD + k
                        if start % RING == node_slot:
                            pool.wait_ge(q_stored, 16 * NQ)
                        if start % RING == splits_slot:
                            pool.wait_ge(stack_stored, 16 * len(STACK))
                        gather(start % RING, p_table, gather_done[start % 4])
                        pool.wait_ge(gather_done[(RAW + k) % 4], r * (64 * RING // 4) + 64 * (k // 4 + 1))
                        pool.wait_ge(slot_free, r * RING + (start + 2))
                        pool.sem_inc(gathered, 1)
                for g in range(RAW + ROUNDS * RING, NG):
                    if g + AHEAD < NG:
                        pool.wait_ge(slot_free, g + AHEAD + 1)
                        gather((g + AHEAD) % RING, p_table, gather_done[(g + AHEAD) % 4], tiles(0, g + AHEAD))
                    pool.wait_ge(gather_done[g % 4], 64 * ((g - RAW) // 4) + 16 * tiles(0, g))
                    pool.sem_inc(gathered, 1)
            with pool.Else():
                pool.wait_ge(q_stored, 16 * NQ)
                pool.wait_ge(p_kept, NQ + RAW)
                with pool.Fori(0, NG) as g:
                    pool.wait_ge(gen_turn, g + 1)
                    pool.wait_ge(gen_dst, g * 32 + 32)
                    pool.sem_inc(gen_claimed, 1)
                    for t in range(TPG):
                        row_gather(t, p_table, src_slots[:, t:t + 1], gen_rows)
                        row_gather(TPG + t, q_table, dst_i2[:, t:t + 1], gen_rows)

        @block.scalar
        def _(act):
            act.dma_start(src_slots[:, RAW * TPG:RING * TPG], src_cols[:, RAW * TPG:RING * TPG]).then_inc(src_in, 16)
            act.dma_start(src_later[:, :], src_cols[:, RING * TPG:IDX_W]).then_inc(src_in, 16)
            act.dma_start(pk[:, :], packed).then_inc(consts_in, 16)
            act.dma_start(we5[:, :], w_edge).then_inc(we_in, 16)
            act.dma_start(dst_i[:, 0:NTILES], dst_cols).then_inc(dst_in, 16)
            act.dma_start(base_b[:, :], group_base.partition_broadcast(P)).then_inc(dst_in, 16)

            def keep_h(q):
                act.wait_ge(z_turned, q + 1)
                nc.scalar.activation(h_of(q)[0:C, :], turned(q), ACT.Relu).then_inc(h_kept, 1)

            def keep_p(q):
                act.wait_ge(p_made, q + 1)
                nc.scalar.copy(rows_of(q).rearrange("p b c -> p (b c)"), pc[:, q % 2, 0:C * quad(q)]).then_inc(p_kept, 1)

            def split(s):
                act.wait_ge(split_step, 2 * s) if s else act.wait_ge(edge_in, 16)
                nc.scalar.copy(splits[:, s, :], edge_f).then_inc(split_step, 1)

            def keep_quads(c):
                for q in ln_quads(c):
                    keep_h(q)
                    if q > 0:
                        keep_p(q - 1)
                if q == NQ - 1:
                    keep_p(q)

            def ln_root(c):
                _, b0, n = ln_blocks(c)
                act.wait_ge(ln_var, c + 1)
                nc.scalar.sqrt(ln_w[:, 3, b0:b0 + n], ln_w[:, 2, b0:b0 + n]).then_inc(ln_sqrt, 1)

            ln_root(0)
            for c in range(N_LN):
                rows, b0, n = ln_blocks(c)
                act.wait_ge(z_scales, c + 1)
                for b in range(ln_by_act(c)):
                    last = nc.scalar.activation(rows[:, b, :], rows[:, b, :], ACT.Identity,
                                                bias=ln_shift[:, b0 + b:b0 + b + 1],
                                                scale=ln_rstd[:, b0 + b:b0 + b + 1])
                last.then_inc(z_by_act, 1)
                if c + 1 < N_LN:
                    ln_root(c + 1)
                if c > 0:
                    keep_quads(c - 1)
                if c == N_LN - 2:
                    split(0)
                if c == N_LN - 1:
                    keep_quads(c)
            split(1)
            split(2)
            for c in range(N_LN, N_LN + N_RAW_EARLY):
                ln_root(c)
            act.wait_ge(rows_cleared, 1)
            act.wait_ge(we_ready, 1)
            for k, (_, part) in enumerate(STACK):
                act.dma_start(we_stack[k * EROWS:(k + 1) * EROWS, :],
                              we_split[:, ("hi", "mid", "lo").index(part), :]).then_inc(we_placed, 16)
            act.wait_ge(p_stored, 16 * NQ)
            act.wait_ge(split_step, 5)

            def p1_unit(i, k):
                u = i * 4 + k
                act.wait_ge(p1_lin, u + 1)
                wait(act, p1_stat, u - 1)
                nc.scalar.activation(r_sb[0:C, k % 2, :], (pa, pb)[k % 2][0:C, :, :].rearrange("c a b -> c (a b)"),
                                     ACT.Relu).then_inc(p1_relu, 1)
                if k == 1:
                    for c in p1_raw_ln(i):
                        ln_root(c)
                for q in p1_raw_turn(i, k):
                    keep_h(q)
                for q in p1_raw_table(i, k):
                    keep_p(q)
                for q in p1_quads(i, k):
                    act.wait_ge(q_made, q + 1)
                    nc.scalar.copy(rows_of(q).rearrange("p b c -> p (b c)"),
                                   pc[:, q % 2, 0:C * quad(q)]).then_inc(q_kept, 1)

            def p1_body(i, units=4):
                for k in range(units):
                    p1_unit(i, k)
                act.wait_ge(node_made, i + 1)
                nc.scalar.activation(node_t[:, bass.ds(i * MLP_CHUNK, MLP_CHUNK)], pd[0:C, 0, 0:MLP_CHUNK], ACT.Relu,
                                     bias=vec[:, B_NODE:B_NODE + 1]).then_inc(node_relu, 1)

            p1_passes(act, p1_body, lambda i: p1_body(i, P1_TAIL))
            act.wait_ge(sqrt_asked, 1)
            nc.scalar.sqrt(sc[:, 4:6], sc[:, 2:4]).then_inc(sqrt_done, 1)

            act.wait_ge(flag_ready, 1)
            outside = act.value_load(flag[0:1, 0:1], min_val=0, max_val=2 * P)
            act.wait_ge(main_ready, 1)
            with act.If(outside < 1):
                def keep_edges(i, j):
                    i, j = at(i, j)
                    if not exists(i, j):
                        return
                    g, n = num(i, j), tiles(i, j) * TILE
                    act.wait_ge(edge_lin, g + 1)
                    wait(act, pre_summed, g - 1)
                    nc.scalar.activation(r_sb[0:M1, j % 2, 0:n], pa[0:M1, j % 2, 0:n], ACT.Relu).then_inc(edge_relu, 1)
                    act.wait_ge(hot_turned, g + 1)
                    nc.scalar.copy(hot_n[0:WIN, j % 2, 0:n], pb_b[0:WIN, j % 2, 0:n]).then_inc(hot_kept, 1)

                def keep_messages(i, j):
                    i, j = at(i, j)
                    if not exists(i, j):
                        return
                    g, n = num(i, j), tiles(i, j)
                    wait(act, win_summed, g - 1)
                    wait(act, acc_added, g - 1)
                    act.wait_ge(pre_added, g + 1)
                    nc.scalar.activation(msg[:, j % 2, 0:n, 0:C],
                                         pc[:, j % 2, 0:n * C].rearrange("p (t c) -> p t c", c=C),
                                         ACT.Relu).then_inc(msg_relu, 1)
                    act.wait_ge(msg_relu, g + 1)
                    nc.scalar.square(msg[:, j % 2, 0:n, M1:MW], msg[:, j % 2, 0:n, 0:C]).then_inc(msg_square, 1)

                keep_edges(0, 0)
                keep_edges(0, 1)
                keep_messages(0, 0)

                def fast(i):
                    for j in range(BODY):
                        keep_edges(i, j + 2)
                        keep_messages(i, j + 1)
                passes(act, fast)
            with act.Else():
                with act.Fori(0, NG) as g:
                    act.wait_ge(gen_lin, g + 1)
                    nc.scalar.activation(r_sb[0:M1, 0, 0:GROUP], pa[0:M1, 0, :], ACT.Relu).then_inc(gen_relu, 1)
                    act.wait_ge(gen_pre, g + 1)
                    nc.scalar.activation(msg[:, 0, :, 0:C], pc[:, 0, 0:TPG * C].rearrange("p (t c) -> p t c", c=C),
                                         ACT.Relu).then_inc(gen_msg, 1)
                    act.wait_ge(gen_msg, g + 1)
                    nc.scalar.square(msg[:, 0, :, M1:MW], msg[:, 0, :, 0:C]).then_inc(gen_square, 1)

            act.wait_ge(sqrt_asked, 2)
            nc.scalar.sqrt(sc[:, 12:13], sc[:, 11:12]).then_inc(sqrt_done, 1)

        @block.tensor
        def _(pe):
            pe.wait_ge(consts_in, 16)

            def turn(q):
                chunk = max(c for c in range(N_LN + N_RAW) if q in ln_quads(c))
                pe.wait_ge(z_ready, chunk + 1)
                if ln_by_act(chunk):
                    pe.wait_ge(z_by_act, chunk + 1)
                wait(pe, h_kept, q - 1 if q < NQ else q)
                for b in range(quad(q)):
                    last = nc.tensor.transpose(turned(q)[:, 128 * b:128 * b + 128], rows_of(q)[:, b, :], ident[:, :])
                last.then_inc(z_turned, 1)

            def table(q, w, made):
                for b in range(quad(q)):
                    last = nc.tensor.matmul(pc[:, q % 2, C * b:C * b + C], h_of(q)[:, 128 * b:128 * b + 128], w[:, :],
                                            start=True, stop=True)
                last.then_inc(made, 1)

            turn(0)
            pe.wait_ge(h_zeroed, 16)
            for q in range(NQ):
                if q + 1 < NQ:
                    turn(q + 1)
                pe.wait_ge(h_kept, q + 1)
                wait(pe, p_kept, q - 1)
                table(q, w1, p_made)
                if q == NQ - 1:
                    pe.wait_ge(bad_ready, 1)
                    nc.tensor.matmul(pd[0:1, 0, 0:2], ones[:, :], bad[:, 2:4], start=True,
                                     stop=True).then_inc(bad_counted, 1)
            pe.wait_ge(p_kept, NQ)
            pe.wait_ge(we_placed, 16 * len(STACK))

            def p1_unit(i, k):
                u = i * 4 + k
                pe.wait_ge(p1_x[k], i * 16 + 16)
                wait(pe, p1_relu, u - 1)
                for half in range(2):
                    last = nc.tensor.matmul((pa, pb)[k % 2][0:M1, half, :], we_stack[:, :],
                                            xs[:, k, half * GROUP:(half + 1) * GROUP], start=True, stop=True)
                last.then_inc(p1_lin, 1)
                for q in p1_raw_turn(i, k):
                    turn(q)
                for q in p1_raw_table(i, k):
                    pe.wait_ge(h_kept, q + 1)
                    pe.wait_ge(p_kept, q - 1)
                    pe.wait_ge(q_kept, NQ)
                    table(q, w1, p_made)
                for q in p1_quads(i, k):
                    wait(pe, q_kept, q - 1)
                    table(q, w2, q_made)

            def p1_body(i, units=4):
                for k in range(units):
                    p1_unit(i, k)
                wait(pe, node_relu, i)
                nc.tensor.matmul(pd[0:C, 0, 0:MLP_CHUNK], wn, h_t[:, bass.ds(i * MLP_CHUNK, MLP_CHUNK)],
                                 start=True, stop=True).then_inc(node_made, 1)

            p1_passes(pe, p1_body, lambda i: p1_body(i, P1_TAIL))
            pe.wait_ge(shift_ready, 1)
            nc.tensor.matmul(pd[0:M1, 0, 0:C], t_col[:, :], w3[:, :], start=True, stop=True).then_inc(shift_made, 1)

            def keep_clock(n):
                for _ in range(n):
                    nc.tensor.matmul(pa[:, 1, :], ident_b[:, :], xs[:, 1, 0:GROUP], start=True, stop=True)

            pe.wait_ge(flag_ready, 1)
            outside = pe.value_load(flag[0:1, 0:1], min_val=0, max_val=2 * P)
            pe.wait_ge(main_ready, 1)
            with pe.If(outside < 1):
                def edges(i, j):
                    i, j = at(i, j)
                    if not exists(i, j):
                        return
                    g, n = num(i, j), tiles(i, j)
                    if j % 2 == 0:
                        pe.wait_ge(x_main[j // 2], i * 16 + 16)
                    wait(pe, edge_relu, g - 1)
                    nc.tensor.matmul(pa[0:M1, j % 2, 0:n * TILE], we_stack[:, :],
                                     xs[:, j // 2, j % 2 * GROUP:j % 2 * GROUP + n * TILE],
                                     start=True, stop=True).then_inc(edge_lin, 1)
                    pe.wait_ge(turn_built, g + 1)
                    wait(pe, hot_kept, g - 1)
                    for t in range(n):
                        last = nc.tensor.transpose(pb_b[0:WIN, j % 2, t * TILE:(t + 1) * TILE], hot_b[:, j, t, :],
                                                   ident_b[:, :])
                    last.then_inc(hot_turned, 1)

                def products(i, j):
                    i, j = at(i, j)
                    if not exists(i, j):
                        return
                    g, n = num(i, j), tiles(i, j)
                    pe.wait_ge(edge_relu, g + 1)
                    pe.wait_ge(hot_kept, g + 1)
                    pe.wait_ge(q_in[j], i * 16 + 16)
                    wait(pe, msg_relu, g - 1)
                    for t in range(n):
                        out = pc[:, j % 2, t * C:(t + 1) * C]
                        nc.tensor.matmul(out, r_sb[:, j % 2, t * TILE:(t + 1) * TILE], w3c[:, :],
                                         start=True, stop=False)
                        last = nc.tensor.matmul(out, hot_n[:, j % 2, t * TILE:(t + 1) * TILE], q_win[:, j, :],
                                                start=False, stop=True)
                    last.then_inc(pre_summed, 1)

                def window_sum(i, j):
                    g, n = num(i, j), tiles(i, j)
                    pe.wait_ge(msg_relu, g + 1)
                    wait(pe, win_added, g - 1)
                    pe.wait_ge(hot_built, g + 1)
                    for t in range(n):
                        last = nc.tensor.matmul(pd[0:M1, j % 2, 0:WIN], msg[:, j % 2, t, 0:M1], hot[:, j, t, :],
                                                start=(t == 0), stop=(t == n - 1))
                    last.then_inc(win_summed, 1)

                edges(0, 0)
                edges(0, 1)
                products(0, 0)

                def fast(i):
                    for j in range(BODY):
                        edges(i, j + 2)
                        products(i, j + 1)
                        if isinstance(i, int) and num(i, j) >= NG - 2:
                            keep_clock(W_GATHER[num(i, j) - (NG - 2)])
                        window_sum(i, j)
                passes(pe, fast)
                keep_clock(W_SUMS)
            with pe.Else():
                with pe.Fori(0, NG) as g:
                    pe.wait_ge(gen_turn, g + 1)
                    pe.wait_ge(gen_x, g * 16 + 16)
                    nc.tensor.matmul(pa[0:M1, 0, :], we_stack[:, :], xs[:, 0, 0:GROUP],
                                     start=True, stop=True).then_inc(gen_lin, 1)
                    pe.wait_ge(gen_relu, g + 1)
                    for t in range(TPG):
                        last = nc.tensor.matmul(pc[:, 0, t * C:(t + 1) * C], r_sb[:, 0, t * TILE:(t + 1) * TILE],
                                                w3c[:, :], start=True, stop=True)
                    last.then_inc(gen_sum, 1)
                    with pe.Fori(0, GEN_WINS) as w:
                        pe.wait_ge(gen_msg, g + 1)
                        pe.wait_ge(gen_hot, g * GEN_WINS + w + 1)
                        for t in range(TPG):
                            last = nc.tensor.matmul(pd[0:M1, 0, 0:WIN], msg[:, 0, t, 0:M1], hot[:, 0, t, :],
                                                    start=(t == 0), stop=(t == TPG - 1))
                        last.then_inc(gen_win, 1)

            pe.wait_ge(messages_done, 1)
            for k, lo in ((0, 0), (1, M1)):
                for t in range(TPG):
                    last = nc.tensor.matmul(pd[0:C, 0, k:k + 1], acc[:, t, lo:lo + C], ones[:, :],
                                            start=(t == 0), stop=(t == TPG - 1))
            last.then_inc(sums_made, 1)
            keep_clock(W_SCALES)
            pe.wait_ge(fold_ready, 1)
            nc.tensor.transpose(pa[0:M1, 0, 0:C], fold[:, :], ident[0:C, 0:C]).then_inc(fold_turned, 1)
            keep_clock(W_DIAG)
            pe.wait_ge(diag_kept, 1)
            for q in range(NQ):
                wait(pe, out_ready, q - 3)
                nc.tensor.matmul(out_bank(q), s_diag[:, :], agg[:, 512 * q:512 * q + nodes(q)],
                                 start=True, stop=True).then_inc(out_made, 1)

        @block.vector
        def _(dve):
            steps = [0]

            def link(ins):
                steps[0] += 1
                ins.then_inc(dve_step, 1)
                dve.wait_ge(dve_step, steps[0])

            V = nc.vector
            dve.sem_inc(slot_free, RING)
            V.memset(acc[:, :, :], 0.0).then_inc(zeroed, 1)
            V.memset(ones[:, :], 1.0)
            V.memset(t_col[:, :], 0.0)
            V.memset(we_stack[:, :], 0.0)
            V.memset(xs[:, :, :], 0.0)
            V.memset(w3c[:, :], 0.0)
            V.memset(q_win[:, :, :], 0.0)
            V.memset(bad[:, :], 0.0)

            def ln_stats(c):
                rows, b0, n = ln_blocks(c)
                if c < N_LN:
                    dve.wait_ge(x_in[c], 16)
                else:
                    dve.wait_ge(raw_done[c - N_LN], 16 * RAW_CHUNK * TPG)
                for b in range(n):
                    last = V.bn_stats(ln_st[:, b0 + b, :], rows[:, b, :])
                link(last)
                st, w = ln_st[:, b0:b0 + n, :], ln_w[:, :, b0:b0 + n]
                V.tensor_tensor(w[:, 4, :], st[:, :, 1], st[:, :, 4], ALU.add)
                V.tensor_tensor(w[:, 1, :], st[:, :, 2], st[:, :, 5], ALU.add)
                link(V.tensor_tensor(w[:, 0, :], st[:, :, 1], st[:, :, 4], ALU.subtract))
                link(V.tensor_tensor(w[:, 0, :], w[:, 0, :], w[:, 0, :], ALU.mult))
                link(V.scalar_tensor_tensor(w[:, 1, :], w[:, 0, :], C / 4.0, w[:, 1, :], ALU.mult, ALU.add))
                V.tensor_scalar(w[:, 2, :], w[:, 1, :], 1.0 / C, EPS, ALU.mult, ALU.add).then_inc(ln_var, 1)
                V.tensor_scalar(w[:, 4, :], w[:, 4, :], 0.5, None, ALU.mult)

            def ln_apply(c):
                rows, b0, n = ln_blocks(c)
                cols = slice(b0, b0 + n)
                dve.wait_ge(ln_sqrt, c + 1)
                link(V.reciprocal(ln_rstd[:, cols], ln_rstd[:, cols]))
                if ln_by_act(c):
                    V.scalar_tensor_tensor(ln_shift[:, cols], ln_mean[:, cols], -1.0, ln_rstd[:, cols], ALU.mult,
                                           ALU.mult).then_inc(z_scales, 1)
                for b in range(ln_by_act(c), n):
                    last = V.tensor_scalar(rows[:, b, :], rows[:, b, :], ln_mean[:, b0 + b:b0 + b + 1],
                                           ln_rstd[:, b0 + b:b0 + b + 1], ALU.subtract, ALU.mult)
                last.then_inc(z_ready, 1)

            def take_off(s):
                dve.wait_ge(split_step, 2 * s + 1)
                V.tensor_tensor(edge_f, edge_f, splits[:, s, :], ALU.subtract).then_inc(split_step, 1)

            ln_stats(0)
            for c in range(N_LN):
                if c + 1 < N_LN:
                    ln_stats(c + 1)
                ln_apply(c)

            take_off(0)
            dve.wait_ge(we_in, 16)
            dve.wait_ge(consts_in, 16)
            V.tensor_copy(ident_b[:, :], ident[:, :])
            link(V.tensor_copy(we_split[:, 0, :], we5[:, :]))
            link(V.tensor_tensor(we5[:, :], we5[:, :], we_split[:, 0, :], ALU.subtract))
            link(V.tensor_copy(we_split[:, 1, :], we5[:, :]))
            link(V.tensor_tensor(we5[:, :], we5[:, :], we_split[:, 1, :], ALU.subtract))
            V.tensor_copy(we_split[:, 2, :], we5[:, :]).then_inc(we_ready, 1)

            dve.wait_ge(dst_in, 32)
            rel = dst_rel[:, :, :].rearrange("p g t -> p (g t)")
            far = msg[:, :, :, :].rearrange("p a t w -> p (a t w)")[:, 0:NTILES]
            link(V.tensor_tensor(dst_rel[:, :, :], dst_i[:, 0:NTILES].rearrange("p (g t) -> p g t", t=TPG),
                                 base_b[:, :].unsqueeze(2).to_broadcast([P, NG, TPG]), ALU.subtract))
            full = (NG - 1) * TPG + LAST_TILES - 1
            link(V.tensor_scalar(far, rel, -(WIN - 1) / 2.0, None, ALU.add))
            link(V.tensor_tensor(far, far, far, ALU.mult))
            V.tensor_reduce(bad[:, 0:1], far[:, 0:full], AX, ALU.max)
            link(V.tensor_copy(bad[0:LAST_ROWS, 1:2], far[0:LAST_ROWS, full:full + 1]))
            V.tensor_scalar(bad[:, 2:4], bad[:, 0:2], (WIN / 2.0) ** 2, None, ALU.is_gt).then_inc(bad_ready, 1)
            for k in range(2):
                V.memset(msg[:, k, :, C:M1], 1.0)

            V.memset(r_sb[:, :, :], 0.0)
            V.memset(hot_n[:, :, :], 0.0).then_inc(rows_cleared, 1)
            dve.wait_ge(bad_counted, 1)
            V.tensor_reduce(flag[0:1, 0:1], pd[0:1, 0, 0:2], AX, ALU.max).then_inc(flag_ready, 1)
            take_off(1)
            ln_stats(N_LN)
            for c in range(N_LN, N_LN + N_RAW_EARLY):
                if c + 1 < N_LN + N_RAW_EARLY:
                    ln_stats(c + 1)
                ln_apply(c)

            def p1_body(i, units=4):
                for k in range(units):
                    u = i * 4 + k
                    dve.wait_ge(p1_relu, u + 1)
                    for half in range(2):
                        n = LAST_EDGES if isinstance(i, int) and 2 * u + half == NG - 1 else GROUP
                        last = V.bn_stats(edge_st[:, bass.ds(u * 2 + half, 1), :].rearrange("c a s -> c (a s)"),
                                          r_sb[0:C, k % 2, half * GROUP:half * GROUP + n])
                    last.then_inc(p1_stat, 1)
                    for c in p1_raw_ln(i):
                        if k == 1:
                            ln_stats(c)
                        if k == 2:
                            ln_apply(c)
                dve.wait_ge(node_relu, i + 1)
                V.bn_stats(node_st[:, bass.ds(i, 1), :].rearrange("c a s -> c (a s)"),
                           node_t[:, bass.ds(i * MLP_CHUNK, MLP_CHUNK)]).then_inc(node_stat, 1)

            p1_passes(dve, p1_body, lambda i: p1_body(i, P1_TAIL))
            dve.wait_ge(node_stat, P1_LOOPS + 1)
            V.bn_aggr(sc[:, 6:8], node_st[:, :, :].rearrange("c q s -> c (q s)"))
            dve.wait_ge(p1_stat, NG // 2)
            link(V.bn_aggr(sc[:, 0:2], edge_st[:, :, :].rearrange("c g s -> c (g s)")))
            V.tensor_scalar(sc[:, 2:3], sc[:, 1:2], EPS, None, ALU.add)
            V.tensor_scalar(sc[:, 3:4], sc[:, 7:8], EPS, None, ALU.add).then_inc(sqrt_asked, 1)
            dve.wait_ge(sqrt_done, 1)
            link(V.reciprocal(sc[:, 4:6], sc[:, 4:6]))
            V.tensor_tensor(sc[:, 8:9], sc[:, 4:5], vec[:, G_EDGE:G_EDGE + 1], ALU.mult)
            link(V.tensor_tensor(sc[:, 10:11], sc[:, 5:6], vec[:, G_NODE:G_NODE + 1], ALU.mult))
            V.tensor_scalar(w3c[0:C, :], w3[:, :], sc[:, 8:9], None, ALU.mult)
            V.tensor_tensor(sc[:, 9:10], sc[:, 0:1], sc[:, 8:9], ALU.mult)
            link(V.tensor_tensor(sc[:, 13:14], sc[:, 6:7], sc[:, 10:11], ALU.mult))
            V.tensor_tensor(t_col[:, C:M1], vec[:, BT_EDGE:BT_EDGE + 1], sc[:, 9:10],
                            ALU.subtract).then_inc(shift_ready, 1)
            link(V.tensor_tensor(sc[:, 14:15], vec[:, BT_NODE:BT_NODE + 1], sc[:, 13:14], ALU.subtract))
            V.memset(fold[:, :], 0.0)
            dve.wait_ge(agg_zeroed, 16)
            dve.wait_ge(p_kept, NQ + RAW)
            dve.wait_ge(shift_made, 1)
            V.tensor_tensor(w3c[C:M1, :], pd[C:M1, 0, 0:C], bm_row[C:M1, :], ALU.add).then_inc(main_ready, 1)

            def add_node(i):
                n = node_cols(i)
                part = node_t[:, bass.ds(i * NODE_CHUNK, n)]
                dve.wait_ge(res_in, i * 16 + 16)
                V.scalar_tensor_tensor(part, part, sc[:, 10:11], res[:, 0:n], ALU.mult,
                                       ALU.add).then_inc(node_added, 1)

            outside = dve.value_load(flag[0:1, 0:1], min_val=0, max_val=2 * P)
            with dve.If(outside < 1):
                def build_hot(i, j):
                    i, j = at(i, j)
                    if not exists(i, j):
                        return
                    g, n = num(i, j), tiles(i, j)
                    wait(dve, hot_turned, g - 3)
                    rel = dst_rel[:, bass.ds(g, 1), 0:n].rearrange("p a t -> p (a t)").unsqueeze(2).to_broadcast(
                        [P, n, WIN])
                    V.tensor_tensor(hot_b[:, j, 0:n, :], rel, ramp[:, :].unsqueeze(1).to_broadcast([P, n, WIN]),
                                    ALU.is_equal).then_inc(turn_built, 1)
                    wait(dve, win_summed, g - 3)
                    V.tensor_tensor(hot[:, j, 0:n, :], rel, ramp[:, :].unsqueeze(1).to_broadcast([P, n, WIN]),
                                    ALU.is_equal).then_inc(hot_built, 1)

                def add_gathered(i, j):
                    i, j = at(i, j)
                    if not exists(i, j):
                        return
                    g, n = num(i, j), tiles(i, j) * C
                    dve.wait_ge(pre_summed, g + 1)
                    dve.wait_ge(gathered, g + 1)
                    V.tensor_tensor(pc[:, j % 2, 0:n], pc[:, j % 2, 0:n],
                                    ring[:, bass.ds((g % RING) * (TPG * C), n)], ALU.add).then_inc(pre_added, 1)
                    if not isinstance(g, int) or g + RING < NG:
                        dve.wait_ge(src_in, 32)
                        V.tensor_copy(src_slots[:, bass.ds((g % RING) * TPG, TPG)],
                                      src_later[:, bass.ds(g * TPG, TPG)]).then_inc(slot_free, 1)

                def add_sums(i, j, base):
                    g, n = num(i, j), tiles(i, j)
                    dve.wait_ge(msg_square, g + 1)
                    wait(dve, acc_added, g)
                    V.tensor_tensor(acc[:, 0:n, :], acc[:, 0:n, :], msg[:, j % 2, 0:n, :],
                                    ALU.add).then_inc(acc_added, 1)
                    if isinstance(g, int) and g == NG - 1:
                        dve.wait_ge(acc_added, NG)
                        dve.wait_ge(win_added, NG - 1)
                        dve.sem_inc(messages_done, 1)
                    dve.wait_ge(win_summed, g + 1)
                    wait(dve, win_added, g)
                    V.tensor_tensor(agg[:, bass.ds(base, WIN)], agg[:, bass.ds(base, WIN)], pd[0:M1, j % 2, 0:WIN],
                                    ALU.add).then_inc(win_added, 1)

                for j in range(3):
                    build_hot(0, j)
                add_gathered(0, 0)

                def fast(i):
                    for j in range(BODY):
                        base = dve.value_load(base_b[0:1, bass.ds(num(i, j), 1)], min_val=0, max_val=N - 1)
                        build_hot(i, j + 3)
                        add_gathered(i, j + 1)
                        add_sums(i, j, base)
                        if j == 1:
                            add_node(i)
                passes(dve, fast)
            with dve.Else():
                dve.wait_ge(src_in, 32)
                dve.sem_inc(gen_turn, 1)
                far4 = bad[:, 0:TPG]
                with dve.Fori(0, NG) as g:
                    dve.wait_ge(gen_dst, g * 32 + 32)
                    V.tensor_copy(far4, dst_i2[:, 0:TPG]).then_inc(gen_step, 1)
                    dve.wait_ge(gen_sum, g + 1)
                    dve.wait_ge(gen_rows, g * (32 * TPG) + 32 * TPG)
                    per = GEN_WINS * 2 + 3
                    V.tensor_tensor(pc[:, 0, 0:TPG * C], pc[:, 0, 0:TPG * C], ring[:, 0:TPG * C],
                                    ALU.add).then_inc(gen_step, 1)
                    dve.wait_ge(gen_step, g * per + 2)
                    V.tensor_tensor(pc[:, 0, 0:TPG * C], pc[:, 0, 0:TPG * C], ring[:, TPG * C:2 * TPG * C],
                                    ALU.add).then_inc(gen_pre, 1)
                    dve.wait_ge(gen_square, g + 1)
                    V.tensor_tensor(acc[:, :, :], acc[:, :, :], msg[:, 0, :, :], ALU.add).then_inc(gen_step, 1)
                    with dve.Fori(0, GEN_WINS) as w:
                        V.tensor_tensor(hot[:, 0, :, :], far4.unsqueeze(2).to_broadcast([P, TPG, WIN]),
                                        ramp[:, :].unsqueeze(1).to_broadcast([P, TPG, WIN]),
                                        ALU.is_equal).then_inc(gen_hot, 1)
                        dve.wait_ge(gen_win, g * GEN_WINS + w + 1)
                        V.tensor_scalar(far4, far4, -float(WIN), None, ALU.add).then_inc(gen_step, 1)
                        V.tensor_tensor(agg[:, bass.ds(w * WIN, WIN)], agg[:, bass.ds(w * WIN, WIN)],
                                        pd[0:M1, 0, 0:WIN], ALU.add).then_inc(gen_step, 1)
                        dve.wait_ge(gen_step, g * per + w * 2 + 5)
                    V.memset(flag[0:1, 0:1], 0).then_inc(gen_turn, 1)
                dve.wait_ge(gen_turn, NG + 1)
                passes(dve, add_node)
                dve.sem_inc(messages_done, 1)

            dve.wait_ge(sums_made, 1)
            link(V.tensor_scalar(sc[:, 0:2], pd[0:C, 0, 0:2], 1.0 / E, None, ALU.mult))
            link(V.tensor_tensor(sc[:, 2:3], sc[:, 0:1], sc[:, 0:1], ALU.mult))
            link(V.tensor_tensor(sc[:, 3:4], sc[:, 1:2], sc[:, 2:3], ALU.subtract))
            V.tensor_scalar(sc[:, 11:12], sc[:, 3:4], 0.0, EPS, ALU.max, ALU.add).then_inc(sqrt_asked, 1)
            dve.wait_ge(sqrt_done, 2)
            link(V.reciprocal(sc[:, 12:13], sc[:, 12:13]))
            link(V.tensor_tensor(sc[:, 8:9], sc[:, 12:13], vec[:, G_MSG:G_MSG + 1], ALU.mult))
            V.tensor_scalar(fold[:, 0:C], ident[0:C, 0:C], sc[:, 8:9], None, ALU.mult)
            link(V.tensor_tensor(sc[:, 9:10], sc[:, 0:1], sc[:, 8:9], ALU.mult))
            V.tensor_tensor(fold[:, C:M1], vec[:, BT_MSG:BT_MSG + 1], sc[:, 9:10],
                            ALU.subtract).then_inc(fold_ready, 1)
            dve.wait_ge(fold_turned, 1)
            V.tensor_copy(s_diag[:, :], pa[0:M1, 0, 0:C]).then_inc(diag_kept, 1)
            dve.wait_ge(node_added, LOOPS)
            for q in range(NQ):
                dve.wait_ge(out_made, q + 1)
                part = node_t[:, 512 * q:512 * q + nodes(q)]
                V.scalar_tensor_tensor(part, out_bank(q), sc[:, 14:15], part, ALU.add,
                                       ALU.add).then_inc(out_ready, 1)


def kernel(**inputs):
    import numpy as _np
    import concourse.bacc as _bacc
    from concourse import mybir as _mybir
    from concourse.bass_utils import run_bass_kernel_spmd as _run

    x, src, dst, ea = (_np.asarray(inputs[k]) for k in ("x", "src", "dst", "edge_attr_4"))
    w = {k[7:]: _np.asarray(v) for k, v in inputs.items() if k.startswith("L0_gnn_")}
    x_pad = _np.zeros((NP, C), x.dtype)
    x_pad[:N] = x
    src_pad = _np.full(IDX_W * TILE, N, src.dtype)
    src_pad[:E] = src
    dst_pad = _np.full(EP, N, dst.dtype)
    dst_pad[:E] = dst
    rows = _np.zeros((EROWS, EP), ea.dtype)
    rows[0, :E] = 1.0
    rows[1:, :E] = ea.T
    packed = _np.zeros((P, PACKED), _np.float32)
    packed[:, 0:P] = _np.eye(P)
    packed[:, RAMP_AT:RAMP_AT + WIN] = _np.arange(WIN)
    for k, part in enumerate((w["W_node"], w["W_msg"][:C], w["W_msg"][C:2 * C], w["W_msg"][2 * C:])):
        packed[:C, WN_AT + k * C:WN_AT + (k + 1) * C] = part
    packed[C, BM_AT:BM_AT + C] = w["b_msg"]
    for k, name in enumerate(("b_node", "g_node", "beta_node", "g_edge", "beta_edge", "g_msg", "beta_msg")):
        packed[:C, VEC_AT + k] = w[name]
    w_edge = _np.zeros((EROWS, M1), _np.float32)
    w_edge[0, :C] = w["b_edge"]
    w_edge[0, C] = 1.0
    w_edge[1:, :C] = w["W_edge"]
    arrays = {
        "x_rows": x,
        "x_nodes": x_pad.reshape(NB, P, C).transpose(1, 0, 2),
        "x_t": x.T,
        "src_cols": src_pad.reshape(IDX_W, TILE).T,
        "dst_cols": dst_pad.reshape(NTILES, TILE).T,
        "group_base": dst_pad[::GROUP],
        "edge_rows": rows.reshape(P, SPLIT_F),
        "packed": packed,
        "w_edge": w_edge,
    }
    nc = _bacc.Bacc("TRN2", target_bir_lowering=False, num_devices=1)
    args = []
    for name in list(arrays):
        a = arrays["in_" + name] = _np.ascontiguousarray(arrays.pop(name))
        args.append(nc.dram_tensor("in_" + name, a.shape, _mybir.dt.from_np(a.dtype), kind="ExternalInput").ap())
    args.append(nc.dram_tensor("out_t", (C, N), _mybir.dt.float32, kind="ExternalOutput").ap())
    graph_layer(nc, *args)
    r = _run(nc, [arrays], core_ids=[0])
    return _np.ascontiguousarray(r.results[0]["out_t"].T)
```
